# Optimizing a Trainium2 kernel written in Bass

```python
import numpy as np
import jax
import jax.numpy as jnp

def _softmax(x, axis=-1):
    return jax.nn.softmax(x, axis=axis)

def _gelu(x):
    return jax.nn.gelu(x, approximate=True)

def _silu(x):
    return jax.nn.silu(x)

def _sigmoid(x):
    return jax.nn.sigmoid(x)

def _layernorm(x, axis=-1, eps=1e-05):
    m = jnp.mean(x, axis=axis, keepdims=True)
    v = jnp.var(x, axis=axis, keepdims=True)
    return (x - m) / jnp.sqrt(v + eps)

def _scatter_add(tgt, idx, src, axis=0):
    return tgt.at[idx].add(src)

def _segment_sum(src, seg, n):
    return jax.ops.segment_sum(src, seg, n)
kernel_name = 'mk_flamingo_gated_d2_seqx_r4_fb84e5'

def setup_inputs(seed: int=0):
    np.random.seed(seed)
    _w = jnp.asarray

    def _rec_inputs():
        import jax
        import jax.numpy as jnp
        _rk = jax.random.key(seed)
        x = -0.0002928 + 1 * jax.random.normal(jax.random.fold_in(_rk, 1), (16, 100, 512), jnp.float32)
        _lenS = 100 - jax.random.randint(jax.random.fold_in(_rk, 7), (16,), 0, max(1, 100 // 4) + 1, jnp.int32)
        _lenS2 = 361 - jax.random.randint(jax.random.fold_in(_rk, 8), (16,), 0, max(1, 361 // 4) + 1, jnp.int32)
        _ctx_512P = jax.random.normal(jax.random.fold_in(_rk, 11), (16, 16, 128), jnp.float32)
        _ctx_512c = jax.random.dirichlet(jax.random.fold_in(_rk, 511), 0.3 * jnp.ones((16,), jnp.float32), (16, 361))
        _ctx_512t = jnp.einsum('bsk,bkd->bsd', _ctx_512c, _ctx_512P)
        _ctx_512t = _ctx_512t * jax.lax.rsqrt(jnp.mean(jnp.square(_ctx_512t)) + 1e-12) * 0.953939
        ctx_512 = 0.000227908 + 0.99994 * (_ctx_512t + 0.3 * jax.random.normal(jax.random.fold_in(_rk, 611), (16, 361, 128), jnp.float32))
        _g = jax.random.normal(jax.random.fold_in(_rk, 9001), (2, 2), jnp.float32)
        _g = jnp.sign(_g) * jnp.maximum(jnp.abs(_g), 1.0) + (_g == 0) * 1.0
        g_xattn = _g[0]
        g_ffn = _g[1]
        return (x, ctx_512, g_xattn, g_ffn)
    x, ctx_512, g_xattn, g_ffn = _rec_inputs()

    def _L0_xattn_setup():
        import jax, jax.numpy as jnp
        import numpy as np
        B, S, L = (2, 256, 256)
        DIM_Q, H, K, D_C, D_CQ, R = (512, 16, 128, 128, 384, 64)

        def _rope_tables(length, dim):
            inv = 1.0 / 10000.0 ** (jnp.arange(0, dim, 2, dtype=jnp.float32) / dim)
            f = jnp.arange(length, dtype=jnp.float32)[:, None] * inv[None, :]
            sin = jnp.repeat(jnp.sin(f), 2, axis=-1)
            cos = jnp.repeat(jnp.cos(f), 2, axis=-1)
            return (sin, cos)

        def _rotate_half(x):
            half = x.shape[-1] // 2
            return jnp.concatenate([-x[..., half:], x[..., :half]], axis=-1)

        def _apply_rope(x, sin, cos):
            return x * cos + _rotate_half(x) * sin
        key = jax.random.key(seed)
        ks = jax.random.split(key, 8)
        return {'hidden_q': jax.random.normal(ks[0], (B, S, DIM_Q), jnp.float32), 'kv_c': jax.random.normal(ks[1], (B, L, D_C), jnp.float32), 'Wq': jax.random.normal(ks[2], (H * K, DIM_Q), jnp.float32) / np.sqrt(DIM_Q).astype(np.float32), 'w_kc_q': jax.random.normal(ks[3], (H, K, D_CQ), jnp.float32) / np.sqrt(K).astype(np.float32), 'w_kc_kv': jax.random.normal(ks[4], (H, K, D_C), jnp.float32) / np.sqrt(K).astype(np.float32), 'W_qr': jax.random.normal(ks[5], (H, D_CQ, R), jnp.float32) / np.float32(np.sqrt(D_CQ) * np.sqrt(R)), 'W_kr': jax.random.normal(ks[6], (H, D_C, R), jnp.float32) / np.sqrt(D_C).astype(np.float32), 'Wo': jax.random.normal(ks[7], (DIM_Q, H * K), jnp.float32) / np.sqrt(H * K).astype(np.float32)}
    _L0_xattn_all = _L0_xattn_setup()
    _L0_xattn_in = {k: v for k, v in _L0_xattn_all.items() if k in ('Wq', 'w_kc_q', 'w_kc_kv', 'W_qr', 'W_kr', 'Wo')}
    del _L0_xattn_all

    def _L0_ffn_setup():
        import jax, jax.numpy as jnp
        import numpy as np
        EPS = 1e-05

        def _quant_weight(w):
            scale = jnp.mean(jnp.abs(w)) + EPS
            wq = jnp.clip(jnp.round(w / scale), -1.0, 1.0)
            return (wq, scale)

        def _quant_act(x):
            s = jnp.max(jnp.abs(x), axis=-1, keepdims=True) / 127.0 + EPS
            xq = jnp.clip(jnp.round(x / s), -128.0, 127.0)
            return (xq, s)

        def _qlinear(x, w):
            wq, ws = _quant_weight(w)
            xq, xs = _quant_act(x)
            y = jnp.einsum('bsi,oi->bso', xq, wq)
            return y * xs * ws
        key = jax.random.key(seed)
        k1, k2, k3, k4 = jax.random.split(key, 4)
        H, I = (512, 2048)
        x = jax.random.normal(k1, (4, 1024, H), dtype=jnp.float32)
        w_gate = jax.random.normal(k2, (I, H), dtype=jnp.float32) * (1.0 / np.sqrt(H))
        w_up = jax.random.normal(k3, (I, H), dtype=jnp.float32) * (1.0 / np.sqrt(H))
        w_down = jax.random.normal(k4, (H, I), dtype=jnp.float32) * (1.0 / np.sqrt(I))
        return {'x': x, 'w_gate': w_gate, 'w_up': w_up, 'w_down': w_down}
    _L0_ffn_all = _L0_ffn_setup()
    _L0_ffn_in = {k: v for k, v in _L0_ffn_all.items() if k in ('w_gate', 'w_up', 'w_down')}
    del _L0_ffn_all

    def _L1_xattn_setup():
        import jax, jax.numpy as jnp
        import numpy as np
        B, S, H, NH, L = (2, 512, 512, 16, 128)
        HD = H // NH
        key = jax.random.key(seed)
        k1, k2, k3, k4, k5 = jax.random.split(key, 5)
        scale = 0.02
        return {'q': jax.random.normal(k1, (B, S, H), dtype=jnp.float32), 'latent_kv': jax.random.normal(k2, (B, S, L), dtype=jnp.float32), 'Wq': jax.random.normal(k3, (H, H), dtype=jnp.float32) * scale, 'Wkv_expand': jax.random.normal(k4, (2 * H, L), dtype=jnp.float32) * scale, 'Wout': jax.random.normal(k5, (H, H), dtype=jnp.float32) * scale}
    _L1_xattn_all = _L1_xattn_setup()
    _L1_xattn_in = {k: v for k, v in _L1_xattn_all.items() if k in ('Wq', 'Wkv_expand', 'Wout')}
    del _L1_xattn_all

    def _L1_ffn_setup():
        import jax, jax.numpy as jnp
        import numpy as np
        H = 512
        I = 512
        E_ROUTED = 7
        NS = 1
        TOPK = 2
        TEMP = 1.0

        def _moe_forward(x, Wr, br, gate_bias, Wup, bup, Wgate, bgate, Wdown, bdown, Wsu, bsu, Wsg, bsg, Wsd, bsd):
            B, S, _ = x.shape
            xt = x.reshape(-1, H)
            N = xt.shape[0]
            gate = (xt @ Wr + br) / TEMP
            bias_gate = gate + gate_bias
            _, ids = jax.lax.top_k(bias_gate, TOPK)
            sel_logits = jnp.take_along_axis(gate, ids, axis=-1)
            masked = jnp.full_like(gate, -jnp.inf)
            masked = masked.at[jnp.arange(N)[:, None], ids].set(sel_logits)
            probs = jax.nn.softmax(masked, axis=-1)
            u = jnp.einsum('nh,ehi->eni', xt, Wup) + bup[:, None, :]
            g = jax.nn.silu(jnp.einsum('eni,eij->enj', u, Wgate) + bgate[:, None, :]) * u
            eo = jnp.einsum('enj,ejh->enh', g, Wdown) + bdown[:, None, :]
            out = jnp.einsum('ne,enh->nh', probs, eo)
            su = (xt @ Wsu + bsu).reshape(N, NS, I)
            sg = jax.nn.silu(su @ Wsg + bsg) * su
            so = (sg @ Wsd + bsd).sum(axis=1)
            out = out + so
            return out.reshape(B, S, H)
        key = jax.random.key(seed)
        ks = jax.random.split(key, 20)
        s = lambda fan_in: 1.0 / np.sqrt(fan_in)
        inp = {'x': jax.random.normal(ks[0], (4, 256, H), dtype=jnp.float32), 'Wr': jax.random.normal(ks[1], (H, E_ROUTED), jnp.float32) * s(H), 'br': jax.random.normal(ks[2], (E_ROUTED,), jnp.float32) * s(H), 'gate_bias': jnp.zeros((E_ROUTED,), jnp.float32), 'Wup': jax.random.normal(ks[3], (E_ROUTED, H, I), jnp.float32) * s(H), 'bup': jax.random.normal(ks[4], (E_ROUTED, I), jnp.float32) * s(H), 'Wgate': jax.random.normal(ks[5], (E_ROUTED, I, I), jnp.float32) * s(I), 'bgate': jax.random.normal(ks[6], (E_ROUTED, I), jnp.float32) * s(I), 'Wdown': jax.random.normal(ks[7], (E_ROUTED, I, H), jnp.float32) * s(I), 'bdown': jax.random.normal(ks[8], (E_ROUTED, H), jnp.float32) * s(I), 'Wsu': jax.random.normal(ks[9], (H, NS * I), jnp.float32) * s(H), 'bsu': jax.random.normal(ks[10], (NS * I,), jnp.float32) * s(H), 'Wsg': jax.random.normal(ks[11], (I, I), jnp.float32) * s(I), 'bsg': jax.random.normal(ks[12], (I,), jnp.float32) * s(I), 'Wsd': jax.random.normal(ks[13], (I, H), jnp.float32) * s(I), 'bsd': jax.random.normal(ks[14], (H,), jnp.float32) * s(I)}
        return inp
    _L1_ffn_all = _L1_ffn_setup()
    _L1_ffn_in = {k: v for k, v in _L1_ffn_all.items() if k in ('Wr', 'br', 'gate_bias', 'Wup', 'bup', 'Wgate', 'bgate', 'Wdown', 'bdown', 'Wsu', 'bsu', 'Wsg', 'bsg', 'Wsd', 'bsd')}
    del _L1_ffn_all
    return {'x': x, 'ctx_512': ctx_512, 'g_xattn': g_xattn, 'g_ffn': g_ffn, 'L0_xattn_Wq': _L0_xattn_in['Wq'], 'L0_xattn_w_kc_q': _L0_xattn_in['w_kc_q'], 'L0_xattn_w_kc_kv': _L0_xattn_in['w_kc_kv'], 'L0_xattn_W_qr': _L0_xattn_in['W_qr'], 'L0_xattn_W_kr': _L0_xattn_in['W_kr'], 'L0_xattn_Wo': _L0_xattn_in['Wo'], 'L0_ffn_w_gate': _L0_ffn_in['w_gate'], 'L0_ffn_w_up': _L0_ffn_in['w_up'], 'L0_ffn_w_down': _L0_ffn_in['w_down'], 'L1_xattn_Wq': _L1_xattn_in['Wq'], 'L1_xattn_Wkv_expand': _L1_xattn_in['Wkv_expand'], 'L1_xattn_Wout': _L1_xattn_in['Wout'], 'L1_ffn_Wr': _L1_ffn_in['Wr'], 'L1_ffn_br': _L1_ffn_in['br'], 'L1_ffn_gate_bias': _L1_ffn_in['gate_bias'], 'L1_ffn_Wup': _L1_ffn_in['Wup'], 'L1_ffn_bup': _L1_ffn_in['bup'], 'L1_ffn_Wgate': _L1_ffn_in['Wgate'], 'L1_ffn_bgate': _L1_ffn_in['bgate'], 'L1_ffn_Wdown': _L1_ffn_in['Wdown'], 'L1_ffn_bdown': _L1_ffn_in['bdown'], 'L1_ffn_Wsu': _L1_ffn_in['Wsu'], 'L1_ffn_bsu': _L1_ffn_in['bsu'], 'L1_ffn_Wsg': _L1_ffn_in['Wsg'], 'L1_ffn_bsg': _L1_ffn_in['bsg'], 'L1_ffn_Wsd': _L1_ffn_in['Wsd'], 'L1_ffn_bsd': _L1_ffn_in['bsd']}

def reference(x, ctx_512, g_xattn, g_ffn, L0_xattn_Wq, L0_xattn_w_kc_q, L0_xattn_w_kc_kv, L0_xattn_W_qr, L0_xattn_W_kr, L0_xattn_Wo, L0_ffn_w_gate, L0_ffn_w_up, L0_ffn_w_down, L1_xattn_Wq, L1_xattn_Wkv_expand, L1_xattn_Wout, L1_ffn_Wr, L1_ffn_br, L1_ffn_gate_bias, L1_ffn_Wup, L1_ffn_bup, L1_ffn_Wgate, L1_ffn_bgate, L1_ffn_Wdown, L1_ffn_bdown, L1_ffn_Wsu, L1_ffn_bsu, L1_ffn_Wsg, L1_ffn_bsg, L1_ffn_Wsd, L1_ffn_bsd):
    import jax
    import jax.numpy as jnp

    def _L0_xattn_ref(hidden_q, kv_c, Wq, w_kc_q, w_kc_kv, W_qr, W_kr, Wo):
        import jax, jax.numpy as jnp
        import numpy as np
        B, S, L = (2, 256, 256)
        DIM_Q, H, K, D_C, D_CQ, R = (512, 16, 128, 128, 384, 64)

        def _rope_tables(length, dim):
            inv = 1.0 / 10000.0 ** (jnp.arange(0, dim, 2, dtype=jnp.float32) / dim)
            f = jnp.arange(length, dtype=jnp.float32)[:, None] * inv[None, :]
            sin = jnp.repeat(jnp.sin(f), 2, axis=-1)
            cos = jnp.repeat(jnp.cos(f), 2, axis=-1)
            return (sin, cos)

        def _rotate_half(x):
            half = x.shape[-1] // 2
            return jnp.concatenate([-x[..., half:], x[..., :half]], axis=-1)

        def _apply_rope(x, sin, cos):
            return x * cos + _rotate_half(x) * sin
        Bv, Sv, _ = hidden_q.shape
        _, Lv, _ = kv_c.shape
        q_hk = (hidden_q @ Wq.T).reshape(Bv, Sv, H, K)
        q_big = jnp.einsum('bshk,hkq->bshq', q_hk, w_kc_q)
        sin_q, cos_q = _rope_tables(Sv, D_CQ)
        q_big = _apply_rope(q_big, sin_q[None, :, None, :], cos_q[None, :, None, :])
        sin_k, cos_k = _rope_tables(Lv, D_C)
        kv_r = _apply_rope(kv_c, sin_k[None], cos_k[None])
        q_r = jnp.einsum('bshq,hqr->bhsr', q_big, W_qr)
        k_r = jnp.einsum('bld,hdr->bhlr', kv_r, W_kr)
        scores = jnp.einsum('bhsr,bhlr->bhsl', q_r, k_r)
        attn = jax.nn.softmax(scores, axis=-1)
        ctx_c = jnp.einsum('bhsl,bld->bhsd', attn, kv_r)
        ctx_lat = jnp.einsum('bhsd,hkd->bhsk', ctx_c, w_kc_kv)
        ctx = ctx_lat.transpose(0, 2, 1, 3).reshape(Bv, Sv, H * K)
        return ctx @ Wo.T

    def _L0_ffn_ref(x, w_gate, w_up, w_down):
        import jax, jax.numpy as jnp
        import numpy as np
        EPS = 1e-05

        def _quant_weight(w):
            scale = jnp.mean(jnp.abs(w)) + EPS
            wq = jnp.clip(jnp.round(w / scale), -1.0, 1.0)
            return (wq, scale)

        def _quant_act(x):
            s = jnp.max(jnp.abs(x), axis=-1, keepdims=True) / 127.0 + EPS
            xq = jnp.clip(jnp.round(x / s), -128.0, 127.0)
            return (xq, s)

        def _qlinear(x, w):
            wq, ws = _quant_weight(w)
            xq, xs = _quant_act(x)
            y = jnp.einsum('bsi,oi->bso', xq, wq)
            return y * xs * ws
        gate = jax.nn.silu(_qlinear(x, w_gate))
        up = _qlinear(x, w_up)
        return _qlinear(gate * up, w_down)

    def _L1_xattn_ref(q, latent_kv, Wq, Wkv_expand, Wout):
        import jax, jax.numpy as jnp
        import numpy as np
        B, S, H, NH, L = (2, 512, 512, 16, 128)
        HD = H // NH
        b, sq, _ = q.shape
        sk = latent_kv.shape[1]
        qp = q @ Wq.T
        kv = latent_kv @ Wkv_expand.T
        k, v = jnp.split(kv, 2, axis=-1)
        qh = qp.reshape(b, sq, NH, HD).transpose(0, 2, 1, 3)
        kh = k.reshape(b, sk, NH, HD).transpose(0, 2, 1, 3)
        vh = v.reshape(b, sk, NH, HD).transpose(0, 2, 1, 3)
        inv_sqrt_d = 1.0 / jnp.sqrt(jnp.float32(HD))
        scores = jnp.einsum('bhqd,bhkd->bhqk', qh, kh) * inv_sqrt_d
        causal = jnp.tril(jnp.ones((sq, sk), dtype=bool))
        scores = jnp.where(causal, scores, jnp.finfo(scores.dtype).min)
        attn = jax.nn.softmax(scores, axis=-1)
        out = jnp.einsum('bhqk,bhkd->bhqd', attn, vh)
        out = out.transpose(0, 2, 1, 3).reshape(b, sq, H)
        return out @ Wout.T

    def _L1_ffn_ref(x, Wr, br, gate_bias, Wup, bup, Wgate, bgate, Wdown, bdown, Wsu, bsu, Wsg, bsg, Wsd, bsd):
        import jax, jax.numpy as jnp
        import numpy as np
        H = 512
        I = 512
        E_ROUTED = 7
        NS = 1
        TOPK = 2
        TEMP = 1.0

        def _moe_forward(x, Wr, br, gate_bias, Wup, bup, Wgate, bgate, Wdown, bdown, Wsu, bsu, Wsg, bsg, Wsd, bsd):
            B, S, _ = x.shape
            xt = x.reshape(-1, H)
            N = xt.shape[0]
            gate = (xt @ Wr + br) / TEMP
            bias_gate = gate + gate_bias
            _, ids = jax.lax.top_k(bias_gate, TOPK)
            sel_logits = jnp.take_along_axis(gate, ids, axis=-1)
            masked = jnp.full_like(gate, -jnp.inf)
            masked = masked.at[jnp.arange(N)[:, None], ids].set(sel_logits)
            probs = jax.nn.softmax(masked, axis=-1)
            u = jnp.einsum('nh,ehi->eni', xt, Wup) + bup[:, None, :]
            g = jax.nn.silu(jnp.einsum('eni,eij->enj', u, Wgate) + bgate[:, None, :]) * u
            eo = jnp.einsum('enj,ejh->enh', g, Wdown) + bdown[:, None, :]
            out = jnp.einsum('ne,enh->nh', probs, eo)
            su = (xt @ Wsu + bsu).reshape(N, NS, I)
            sg = jax.nn.silu(su @ Wsg + bsg) * su
            so = (sg @ Wsd + bsd).sum(axis=1)
            out = out + so
            return out.reshape(B, S, H)
        return _moe_forward(x, Wr, br, gate_bias, Wup, bup, Wgate, bgate, Wdown, bdown, Wsu, bsu, Wsg, bsg, Wsd, bsd)
    x = x + jnp.tanh(g_xattn[0]) * _L0_xattn_ref(_layernorm(x, axis=-1), ctx_512, L0_xattn_Wq, L0_xattn_w_kc_q, L0_xattn_w_kc_kv, L0_xattn_W_qr, L0_xattn_W_kr, L0_xattn_Wo)
    x = x + jnp.tanh(g_ffn[0]) * _L0_ffn_ref(_layernorm(x, axis=-1), L0_ffn_w_gate, L0_ffn_w_up, L0_ffn_w_down)
    x = x + jnp.tanh(g_xattn[1]) * _L1_xattn_ref(_layernorm(x, axis=-1), ctx_512, L1_xattn_Wq, L1_xattn_Wkv_expand, L1_xattn_Wout)
    x = x + jnp.tanh(g_ffn[1]) * _L1_ffn_ref(_layernorm(x, axis=-1), L1_ffn_Wr, L1_ffn_br, L1_ffn_gate_bias, L1_ffn_Wup, L1_ffn_bup, L1_ffn_Wgate, L1_ffn_bgate, L1_ffn_Wdown, L1_ffn_bdown, L1_ffn_Wsu, L1_ffn_bsu, L1_ffn_Wsg, L1_ffn_bsg, L1_ffn_Wsd, L1_ffn_bsd)
    return x

_drawn_inputs = setup_inputs


def setup_inputs(seed=0):
    import zlib

    import numpy as np

    out = dict(_drawn_inputs(seed))
    spreads = {'g_ffn': (-1.0, 0.2), 'L1_ffn_gate_bias': (0.0, 0.1)}
    factors = {'L1_xattn_Wq': 5.738, 'L1_ffn_bup': 2.92, 'L1_ffn_bgate': 4.178, 'L1_ffn_bsg': 3.109}
    for name, (base, spread) in spreads.items():
        noise = np.random.default_rng([zlib.crc32(name.encode()), seed]).standard_normal(out[name].shape)
        drawn = base * np.exp(spread * noise) if base else spread * noise
        out[name] = jnp.asarray(drawn.astype(out[name].dtype))
    for name, factor in factors.items():
        out[name] = (out[name] * factor).astype(out[name].dtype)
    return out
```

```python
from contextlib import ExitStack

import concourse.bass as bass
from concourse import mybir
from concourse.alu_op_type import AluOpType as ALU

F32 = mybir.dt.float32
F32R = mybir.dt.float32r
BF16 = mybir.dt.bfloat16
ACT = mybir.ActivationFunctionType
AX = mybir.AxisListType

B, S, D = 16, 100, 512
L, DC = 361, 128
LE = L + L % 2
KC = D // 128
EPS = 1e-5

H0, DK, CQ, R = 16, 128, 384, 64
PAIRS = H0 // 2
CB = CQ // 128
LC, LCN = 121, 3
HB = B // 2
HT = HB * S
NT = 400
GB = NT // S

W_Q, W_KC, W_R = 0, KC * 256, KC * 256 + 2 * CQ
W_KR = W_R + 2 * CB * 2 * R
W_KV = W_KR + DC
W_O = W_KV + 2 * DC
W_ALL = W_O + 2 * D


class Core:

    def __init__(self, nc, ctx):
        self.nc, self.ctx, self.stage_sems = nc, ctx, []
        self.x = self.sbuf("residual", [S, B, D])
        self.ident = self.sbuf("identity", [128, 128])
        self.zero = self.sbuf("zero", [128, 1])
        self.eps = self.sbuf("eps", [128, 1])
        self.gates = self.sbuf("tanh_gates", [128, 4])
        self.mv = self.sbuf("mean_var", [S, B, 2])
        self.rstd = self.sbuf("rstd", [S, B])
        self.nmr = self.sbuf("minus_mean_rstd", [S, B])
        self.stats = self.sbuf("bn_stats", [S, B, 6])
        self.std = self.sbuf("std", [S, B])
        self.ps = ctx.enter_context(nc.psum_tensor("banks", [128, 8, 512], F32))

    def sbuf(self, name, shape, dt=F32, ctx=None):
        return (ctx or self.ctx).enter_context(self.nc.sbuf_tensor(name, shape, dt))

    def sem(self, name):
        s = self.nc.alloc_semaphore(name)
        self.stage_sems.append(s)
        return s

    def end_stage(self):
        self.nc.clear_and_free_semaphores(self.stage_sems)
        self.stage_sems = []
        self.nc.all_engine_barrier()


class NormSems:

    def __init__(self, core, tag):
        self.bn = core.sem(tag + "_bn")
        self.var = core.sem(tag + "_var")
        self.std = core.sem(tag + "_std")
        self.rstd = core.sem(tag + "_rstd")


def norm_stats_dve(dve, core, s, tiles):
    lo, hi = tiles.start, tiles.stop
    n = hi - lo
    for t in tiles:
        dve.bn_stats(core.stats[:, t, :], core.x[:, t, :]).then_inc(s.bn, 1)
    for k, t in enumerate(tiles):
        dve.wait_ge(s.bn, k + 1)
        dve.bn_aggr(core.mv[:, t, :], core.stats[:, t, :]).then_inc(s.var, 1)
    dve.wait_ge(s.std, 1)
    v, y = core.mv[:, lo:hi, 1], core.rstd[:, lo:hi]
    tmp, m = core.std[:, lo:hi], core.nmr[:, lo:hi]
    steps = [
        lambda: dve.reciprocal(y, tmp),
        lambda: dve.tensor_tensor(tmp, y, y, ALU.mult),
        lambda: dve.scalar_tensor_tensor(out=tmp, in0=v, scalar=EPS, in1=tmp, op0=ALU.add, op1=ALU.mult),
        lambda: dve.tensor_scalar(tmp, tmp, -0.5, 1.5, ALU.mult, ALU.add),
        lambda: dve.tensor_tensor(y, y, tmp, ALU.mult),
        lambda: dve.scalar_tensor_tensor(out=m, in0=core.mv[:, lo:hi, 0], scalar=-1.0, in1=y,
                                         op0=ALU.mult, op1=ALU.mult),
    ]
    for k, step in enumerate(steps):
        step().then_inc(s.rstd, 1)
        dve.wait_ge(s.rstd, k + 1)


def norm_stats_act(act, core, s, tiles):
    act.wait_ge(s.var, len(tiles))
    act.activation(core.std[:, tiles.start:tiles.stop], core.mv[:, tiles.start:tiles.stop, 1],
                   ACT.Sqrt, bias=core.eps[0:S, 0:1]).then_inc(s.std, 1)


def latent_attention(core, half, x_in, ctx_in, g_x, g_f, w_pack, rope_q, rope_k, first):
    nc, ps = core.nc, core.ps
    tag = f"la{half}_"
    b0 = half * HB
    tiles = range(b0, b0 + HB)
    with ExitStack() as own:
        def sb(name, shape, dt=F32):
            return core.sbuf(tag + name, shape, dt, own)

        def sem(name):
            return core.sem(tag + name)

        xth = sb("xn_t_high", [128, KC, HT], F32R)
        xtl = sb("xn_t_low", [128, KC, HT], F32R)
        kvh = sb("kv_t_high", [DC, HB, LE], F32R)
        kvl = sb("kv_t_low", [DC, HB, LE], F32R)
        kv = sb("kv_rows", [LC, HB, LCN, DC])
        wts = [sb(f"weights{i}", [128, W_ALL]) for i in range(2)]
        wqh, wql = sb("wq_high", [128, KC, 256], F32R), sb("wq_low", [128, KC, 256], F32R)
        wch, wcl = sb("wkc_high", [128, 2 * CQ], F32R), sb("wkc_low", [128, 2 * CQ], F32R)
        mh, ml = sb("wout_high", [DC, 2, D], F32R), sb("wout_low", [DC, 2, D], F32R)
        qh, ql = sb("q_high", [DK, 2, NT], F32R), sb("q_low", [DK, 2, NT], F32R)
        roped = sb("q_roped", [128, 2, 2, CB, NT])
        rank = sb("q_rank", [2 * R, NT])
        kh, kl = sb("qk_high", [DC, 2, HT], F32R), sb("qk_low", [DC, 2, HT], F32R)
        ch, cl = sb("ctx_high", [DC, 2, 2, S], F32R), sb("ctx_low", [DC, 2, 2, S], F32R)
        prob = sb("probs", [S, 4, LC * LCN])
        probt = sb("probs_t", [LC, 2, LCN, 2, S])
        nmax, sums, rsum = sb("minus_max", [S, 4]), sb("sums", [S, 4]), sb("rsum", [S, 4])
        trig = sb("rope_q", [128, 2, CB, S])
        warm = sb("table_warmer", [1, 1])
        flat = roped[:, :, :, :, :].rearrange("p a b c n -> p (a b c n)")
        raw = flat[0:LC, 0:HB * LCN * DC].rearrange("p (b c d) -> p b c d", b=HB, c=LCN)
        trigk = wts[1][0:LC, 0:2 * LCN * DC].rearrange("p (t c d) -> p t c d", t=2, c=LCN)
        turned = wts[1][0:LC, 2 * LCN * DC:4 * LCN * DC].rearrange("p (i c d) -> p i c d", i=2, c=LCN)
        xn = [wts[1][0:S, 4 * LCN * DC + i * D:4 * LCN * DC + (i + 1) * D] for i in range(2)]

        ns = NormSems(core, tag)
        x_loaded, const_ready = sem("x_loaded"), sem("const_ready")
        pads_zero, kv_loaded, tabs = sem("pads_zero"), sem("kv_loaded"), sem("tables_loaded")
        ident_zero = sem("ident_zero")
        turn, kv_roped = sem("turn"), sem("kv_roped")
        kv_t, kv_high, kv_low = sem("kv_transposed"), sem("kv_high"), sem("kv_low")
        normed, x_t, x_high, x_low = sem("normed"), sem("x_transposed"), sem("x_high"), sem("x_low")
        w_in = [sem(f"weights_in{i}") for i in range(2)]
        w_high, w_split = sem("weights_high"), sem("weights_split")
        w0 = wts[0]
        parts0 = ((w0[:, W_Q:W_KC], wqh[:].rearrange("p k c -> p (k c)"), wql[:].rearrange("p k c -> p (k c)")),
                  (w0[:, W_KC:W_R], wch[:], wcl[:]))
        with nc.Block() as block:
            @block.sync
            def _(sp):
                if first:
                    sp.dma_start(core.x[:], x_in.rearrange("b s d -> s b d")).then_inc(x_loaded, 16)
                sp.wait_ge(pads_zero, 1)
                for c in range(LCN):
                    n = min(LC, L - c * LC)
                    sp.dma_start(raw[0:n, :, c, :],
                                 ctx_in[b0:b0 + HB, c * LC:c * LC + n, :].rearrange("b p d -> p b d")
                                 ).then_inc(kv_loaded, 16)
                sp.dma_start(w0[:], w_pack[0]).then_inc(w_in[0], 16)

            @block.scalar
            def _(act):
                act.dma_start(trigk, rope_k).then_inc(tabs, 16)
                act.dma_start(trig[:], rope_q).then_inc(tabs, 16)
                if first:
                    act.dma_start(core.gates[:, 0:2], g_x.rearrange("(a n) -> a n", a=1)
                                  .to_broadcast([128, 2])).then_inc(tabs, 16)
                    act.dma_start(core.gates[:, 2:4], g_f.rearrange("(a n) -> a n", a=1)
                                  .to_broadcast([128, 2])).then_inc(tabs, 16)
                    act.wait_ge(tabs, 64)
                    act.activation(core.gates[:], core.gates[:], ACT.Tanh).then_inc(const_ready, 1)
                    act.wait_ge(const_ready, 2)
                norm_stats_act(act, core, ns, tiles)
                for i in range(HB):
                    act.wait_ge(x_t, i + 1)
                    act.copy(xth[:, :, i * S:(i + 1) * S],
                             ps[:, i % 2, 0:KC * S].rearrange("p (k s) -> p k s", k=KC)).then_inc(x_high, 1)
                    act.wait_ge(kv_t, i + 1)
                    act.copy(kvh[:, i, 0:L], ps[:, 2 + i % 2, 0:L]).then_inc(kv_high, 1)
                    if i == HB - 3:
                        act.wait_ge(w_in[0], 16)
                        for w, high, _low in parts0:
                            act.copy(high, w).then_inc(w_high, 1)

            @block.gpsimd
            def _(pool):
                pool.memset(raw[:, :, LCN - 1, :], 0.0).then_inc(pads_zero, 1)
                pool.memset(prob[:, :, L:LC * LCN], 0.0)
                pool.memset(kvh[:, :, L:LE].bitcast(F32), 0.0)
                pool.memset(kvl[:, :, L:LE].bitcast(F32), 0.0)
                if first:
                    pool.memset(core.zero[:], 0.0)
                    pool.memset(core.eps[:], EPS).then_inc(const_ready, 1)
                    pool.memset(core.ident[:], 0.0).then_inc(ident_zero, 1)
                    pool.wait_ge(ident_zero, 1)
                    pool.affine_select(out=core.ident[:], in_=core.ident[:], compare_op=ALU.not_equal,
                                       fill=1.0, base=0, pattern=[[-1, 128]],
                                       channel_multiplier=1).then_inc(ident_zero, 1)
                pool.wait_ge(tabs, 32 if not first else 64)
                pool.wait_ge(kv_loaded, 16 * LCN)
                half_d = DC // 2
                for i in range(HB):
                    t = turned[:, i % 2]
                    pool.tensor_tensor(kv[:, i], raw[:, i], trigk[:, 0], ALU.mult).then_inc(turn, 1)
                    pool.tensor_tensor(t[:, :, 0:half_d], raw[:, i, :, half_d:DC],
                                       trigk[:, 1, :, 0:half_d], ALU.mult).then_inc(turn, 1)
                    pool.tensor_tensor(t[:, :, half_d:DC], raw[:, i, :, 0:half_d],
                                       trigk[:, 1, :, half_d:DC], ALU.mult).then_inc(turn, 1)
                    pool.wait_ge(turn, 3 * (i + 1))
                    pool.tensor_tensor(kv[:, i], kv[:, i], t, ALU.add).then_inc(kv_roped, 1)

            def low_parts(dve, i):
                dve.wait_ge(x_high, i + 1)
                dve.tensor_tensor(xtl[:, :, i * S:(i + 1) * S],
                                  ps[:, i % 2, 0:KC * S].rearrange("p (k s) -> p k s", k=KC),
                                  xth[:, :, i * S:(i + 1) * S].bitcast(F32), ALU.subtract).then_inc(x_low, 1)
                dve.wait_ge(kv_high, i + 1)
                dve.tensor_tensor(kvl[:, i, 0:L], ps[:, 2 + i % 2, 0:L], kvh[:, i, 0:L].bitcast(F32),
                                  ALU.subtract).then_inc(kv_low, 1)

            @block.vector
            def _(dve):
                if first:
                    dve.wait_ge(x_loaded, 16)
                norm_stats_dve(dve, core, ns, tiles)
                for i, t in enumerate(tiles):
                    if i >= 2:
                        dve.wait_ge(x_t, i - 1)
                    dve.tensor_scalar(xn[i % 2], core.x[:, t, :], core.rstd[:, t:t + 1],
                                      core.nmr[:, t:t + 1], ALU.mult, ALU.add).then_inc(normed, 1)
                    if i >= 1:
                        low_parts(dve, i - 1)
                for k, (w, high, low) in enumerate(parts0):
                    dve.wait_ge(w_high, k + 1)
                    dve.tensor_tensor(low, w, high.bitcast(F32), ALU.subtract).then_inc(w_split, 1)
                low_parts(dve, HB - 1)

            @block.tensor
            def _(pe):
                if first:
                    pe.wait_ge(ident_zero, 2)
                for i in range(HB):
                    pe.wait_ge(normed, i + 1)
                    if i >= 2:
                        pe.wait_ge(x_low, i - 1)
                    for k in range(KC):
                        mm = pe.transpose(ps[:, i % 2, k * S:(k + 1) * S], xn[i % 2][:, k * 128:(k + 1) * 128],
                                          core.ident[0:S, 0:S])
                    mm.then_inc(x_t, 1)
                    pe.wait_ge(kv_roped, i + 1)
                    if i >= 2:
                        pe.wait_ge(kv_low, i - 1)
                    for c in range(LCN):
                        n = min(LC, L - c * LC)
                        mm = pe.transpose(ps[:, 2 + i % 2, c * LC:c * LC + n], kv[0:n, i, c, :],
                                          core.ident[0:n, 0:n])
                    mm.then_inc(kv_t, 1)

        m_psum, m_high, m_low = sem("wout_psum"), sem("wout_high"), sem("wout_low")
        a_psum, a_high, a_low = sem("q_psum"), sem("q_high"), sem("q_low")
        b_psum, b_done = sem("qbig_psum"), sem("qbig_roped")
        c_psum, c_done, c_block = sem("rank_psum"), sem("rank_out"), sem("rank_blocks")
        k_psum, k_high, k_low = sem("qk_psum"), sem("qk_high"), sem("qk_low")
        s_psum, s_max, s_exp = sem("scores"), sem("scores_max"), sem("scores_exp")
        s_rec, s_norm = sem("rsum"), sem("probs_normed")
        t_psum, t_out = sem("probs_t_psum"), sem("probs_t_out")
        v_psum, v_high, v_low = sem("ctx_psum"), sem("ctx_high"), sem("ctx_low")
        o_psum, o_add = sem("out_psum"), sem("out_added")
        UNITS = 2 * (HT // NT)
        ITEMS = 2 * HB
        MIX, OUT = 5, 8
        SLOTS = OUT + ITEMS - 1
        AHEAD = (SLOTS - 6, SLOTS - 2)
        WIDEN_LAST = (0, 1)
        NARROW = (3, 4)
        ABSORB = 5
        T_BANK, V_BANK, O_BANK = 2, 4, 6
        C_BANKS = (5, O_BANK)
        B_BANKS = (3, 7)
        K_BANKS = ((T_BANK, O_BANK), B_BANKS)

        def wview(par):
            w = wts[par]
            return dict(
                q=w[:, W_Q:W_KC], kc=w[:, W_KC:W_R],
                r=w[:, W_R:W_KR].rearrange("p (v c h r) -> p v c h r", v=2, c=CB, h=2),
                kr=w[:, W_KR:W_KV],
                kv=w[:, W_KV:W_O].rearrange("p (h d) -> p h d", h=2),
                o=w[:, W_O:W_ALL].rearrange("p (h d) -> p h d", h=2))

        with nc.Block() as block:
            @block.sync
            def _(sp):
                sp.dma_start(wts[1][:], w_pack[1]).then_inc(w_in[1], 16)
                with sp.Fori(1, PAIRS // 2) as i:
                    for par in range(2):
                        n = i * 2 + par
                        sp.wait_ge(k_psum, (n - 1) * UNITS)
                        sp.dma_start(wts[par][:], w_pack[n]).then_inc(w_in[par], 16)

            @block.gpsimd
            def _(pool):
                def split(n, i, par):
                    w = wview(par)
                    pool.wait_ge(w_in[par], (i + 1) * 16)
                    pool.wait_ge(a_psum, n * UNITS)
                    pool.tensor_tensor(wqh[:].rearrange("p k c -> p (k c)"), w["q"],
                                       core.zero[:, 0:1].to_broadcast([128, KC * 256]), ALU.add).then_inc(w_high, 1)
                    pool.wait_ge(w_high, n * 2 + 1)
                    pool.tensor_tensor(wql[:].rearrange("p k c -> p (k c)"), w["q"],
                                       wqh[:].rearrange("p k c -> p (k c)").bitcast(F32),
                                       ALU.subtract).then_inc(w_split, 1)
                    pool.wait_ge(b_psum, n * UNITS * CB)
                    pool.tensor_tensor(wch[:], w["kc"], core.zero[:, 0:1].to_broadcast([128, 2 * CQ]),
                                       ALU.add).then_inc(w_high, 1)
                    pool.wait_ge(w_high, n * 2 + 2)
                    pool.tensor_tensor(wcl[:], w["kc"], wch[:].bitcast(F32),
                                       ALU.subtract).then_inc(w_split, 1)

                split(1, 0, 1)
                with pool.Fori(1, PAIRS // 2) as i:
                    for par in range(2):
                        split(i * 2 + par, i, par)

            @block.tensor
            def _(pe):
                def project(n, u, blocks=range(KC)):
                    run, h = u // 2, u % 2
                    if u >= 2 and 0 in blocks:
                        pe.wait_ge(a_low, n * UNITS + u - 1)
                    for k in blocks:
                        xs = slice(run * NT, (run + 1) * NT)
                        wc = slice(h * 128, (h + 1) * 128)
                        for j, (a, b) in enumerate(((wqh, xth), (wqh, xtl), (wql, xth))):
                            mm = pe.matmul(ps[:, u % 2, 0:NT], a[:, k, wc], b[:, k, xs],
                                           start=(k == 0 and j == 0), stop=(k == KC - 1 and j == 2))
                    if KC - 1 in blocks:
                        mm.then_inc(a_psum, 1)

                def widen(n, u, c):
                    h, k = u % 2, u * CB + c
                    if c == 0:
                        pe.wait_ge(a_low, n * UNITS + u + 1)
                    if k >= 2:
                        pe.wait_ge(b_done, (n * UNITS * CB + k - 1) * 2)
                    wc = slice(h * CQ + c * 128, h * CQ + (c + 1) * 128)
                    for j, (a, b) in enumerate(((wch, qh), (wch, ql), (wcl, qh))):
                        mm = pe.matmul(ps[:, B_BANKS[k % 2], 0:NT], a[:, wc], b[:, u % 2, :],
                                       start=(j == 0), stop=(j == 2))
                    mm.then_inc(b_psum, 1)

                def narrow(n, run, w, part, parts):
                    steps = [(v, c) for c in range(CB) for v in range(2)]
                    each = len(steps) // parts
                    if part == 0:
                        pe.wait_ge(b_done, (n * UNITS + 2 * run + 2) * CB * 2)
                    for j in range(part * each, (part + 1) * each):
                        v, c = steps[j]
                        for h in range(2):
                            mm = pe.matmul(ps[h * R:(h + 1) * R, C_BANKS[run], 0:NT], w["r"][:, v, c, h, :],
                                           roped[:, h, v, c, :], start=(j == 0), stop=(j == 2 * CB - 1),
                                           skip_group_check=True)
                        if j == 2 * CB - 1:
                            mm.then_inc(c_psum, 1)
                        elif run == 0 and v == 1:
                            mm.then_inc(c_block, 1)

                def absorb(n, run, w):
                    pe.wait_ge(c_done, n * (UNITS // 2) + run + 1)
                    for h in range(2):
                        pe.matmul(ps[:, K_BANKS[run][h], 0:NT], w["kr"][h * R:(h + 1) * R, :],
                                  rank[h * R:(h + 1) * R, :], start=True, stop=True).then_inc(k_psum, 1)

                def wout(w, h):
                    pe.matmul(ps[:, 4 + h, :], w["kv"][:, h, :], w["o"][:, h, :],
                              start=True, stop=True).then_inc(m_psum, 1)

                def scores(n, j):
                    b, h = j // 2, j % 2
                    pe.wait_ge(k_low, n * UNITS + 2 * (b // GB) + h + 1)
                    if j >= 2:
                        pe.wait_ge(s_exp, n * ITEMS + j - 1)
                    qs = slice(b * S, (b + 1) * S)
                    for k, (a, c) in enumerate(((kh, kvh), (kh, kvl), (kl, kvh))):
                        mm = pe.matmul(ps[0:S, j % 2, 0:LE], a[:, h, qs], c[:, b, :],
                                       start=(k == 0), stop=(k == 2))
                    mm.then_inc(s_psum, 1)

                def turn_probs(n, j):
                    pe.wait_ge(s_norm, n * ITEMS + j + 1)
                    if j >= 1:
                        pe.wait_ge(t_out, n * ITEMS + j)
                    for c in range(LCN):
                        mm = pe.transpose(ps[0:LC, T_BANK, c * S:(c + 1) * S],
                                          prob[:, j % 4, c * LC:(c + 1) * LC], core.ident[0:S, 0:S])
                    mm.then_inc(t_psum, 1)

                def mix(n, b):
                    pe.wait_ge(t_out, n * ITEMS + 2 * b + 2)
                    if b >= 1:
                        pe.wait_ge(v_low, n * HB + b)
                    else:
                        pe.wait_ge(m_low, n * 2 + 1)
                    for c in range(LCN):
                        mm = pe.matmul(ps[:, V_BANK, 0:2 * S], kv[:, b, c, :],
                                       probt[:, b % 2, c, :, :].rearrange("p h s -> p (h s)"),
                                       start=(c == 0), stop=(c == LCN - 1))
                    mm.then_inc(v_psum, 1)

                def out(n, b):
                    pe.wait_ge(v_low, n * HB + b + 1)
                    if b == 0:
                        pe.wait_ge(m_low, n * 2 + 2)
                    else:
                        pe.wait_ge(o_add, n * HB + b)
                    for h in range(2):
                        for j, (a, c) in enumerate(((ch, mh), (ch, ml), (cl, mh))):
                            mm = pe.matmul(ps[0:S, O_BANK, :], a[:, b % 2, h, :], c[:, h, :],
                                           start=(h == 0 and j == 0), stop=(h == 1 and j == 2))
                    mm.then_inc(o_psum, 1)

                def first_units(n, u):
                    pe.wait_ge(w_split, n * 2 + 1)
                    pe.wait_ge(s_exp, n * ITEMS + u - 1)
                    project(n, u)

                def pair(n, i, par, last=False):
                    w = wview(par)
                    pe.wait_ge(w_in[par], (i + 1) * 16)
                    pe.wait_ge(w_split, n * 2 + 2)
                    lo, hi = range(KC // 2), range(KC // 2, KC)
                    widen(n, 0, 0)
                    widen(n, 0, 1)
                    project(n, 2, lo)
                    widen(n, 0, 2)
                    project(n, 2, hi)
                    widen(n, 1, 0)
                    widen(n, 1, 1)
                    project(n, 3, lo)
                    widen(n, 1, 2)
                    project(n, 3, hi)
                    widen(n, 2, 0)
                    widen(n, 2, 1)
                    narrow(n, 0, w, 0, 1)
                    widen(n, 2, 2)
                    wout(w, 0)
                    absorb(n, 0, w)
                    widen(n, 3, 0)
                    wout(w, 1)
                    for s in range(SLOTS):
                        if s < ITEMS:
                            scores(n, s)
                        if s in WIDEN_LAST:
                            widen(n, 3, 1 + WIDEN_LAST.index(s))
                        if s in range(MIX, MIX + ITEMS, 2):
                            mix(n, (s - MIX) // 2)
                        if s == ABSORB:
                            absorb(n, 1, w)
                        if s in range(OUT, OUT + ITEMS, 2):
                            out(n, (s - OUT) // 2)
                        if s in NARROW:
                            narrow(n, 1, w, NARROW.index(s), len(NARROW))
                        if 2 <= s < ITEMS + 2:
                            turn_probs(n, s - 2)
                        if s in AHEAD and not last:
                            first_units(n + 1, AHEAD.index(s))

                project(0, 0)
                project(0, 1)
                with pe.Fori(0, PAIRS // 2 - 1) as i:
                    for par in range(2):
                        pair(i * 2 + par, i, par)
                pair(PAIRS - 2, PAIRS // 2 - 1, 0)
                pair(PAIRS - 1, PAIRS // 2 - 1, 1, last=True)

            @block.scalar
            def _(act):
                def high(n, u):
                    act.wait_ge(a_psum, n * UNITS + u + 1)
                    if u >= 2:
                        act.wait_ge(b_psum, (n * UNITS + u - 1) * CB)
                    act.copy(qh[:, u % 2, :], ps[:, u % 2, 0:NT]).then_inc(a_high, 1)

                def rank_out(n, run):
                    act.wait_ge(c_psum, n * (UNITS // 2) + run + 1)
                    act.copy(rank[:], ps[:, C_BANKS[run], 0:NT]).then_inc(c_done, 1)

                def qk_high(n, run):
                    for h in range(2):
                        act.wait_ge(k_psum, n * UNITS + 2 * run + h + 1)
                        act.copy(kh[:, h, run * NT:(run + 1) * NT],
                                 ps[:, K_BANKS[run][h], 0:NT]).then_inc(k_high, 1)

                def wout_high(n, h):
                    act.wait_ge(m_psum, n * 2 + h + 1)
                    act.activation(mh[:, h, :], ps[:, 4 + h, :], ACT.Copy,
                                   scale=core.gates[:, 0:1]).then_inc(m_high, 1)

                def pair(n, last=False, early=True):
                    if early:
                        act.copy(warm[:], core.zero[0:1, 0:1])
                    high(n, 2)
                    high(n, 3)
                    rank_out(n, 0)
                    qk_high(n, 0)
                    wout_high(n, 0)
                    for s in range(SLOTS):
                        if s < ITEMS:
                            act.wait_ge(s_max, n * ITEMS + s + 1)
                            if s >= 4:
                                act.wait_ge(t_psum, n * ITEMS + s - 3)
                            act.activation(prob[:, s % 4, 0:L], ps[0:S, s % 2, 0:L], ACT.Exp,
                                           bias=nmax[:, s % 4:s % 4 + 1],
                                           accum_out=sums[:, s % 4:s % 4 + 1]).then_inc(s_exp, 1)
                        if s == 0:
                            wout_high(n, 1)
                        if s in range(MIX, MIX + ITEMS, 2):
                            b = (s - MIX) // 2
                            act.wait_ge(v_psum, n * HB + b + 1)
                            if b >= 2:
                                act.wait_ge(o_psum, n * HB + b - 1)
                            act.copy(ch[:, b % 2, :, :].rearrange("p h s -> p (h s)"),
                                     ps[:, V_BANK, 0:2 * S]).then_inc(v_high, 1)
                        if 2 <= s < ITEMS + 2:
                            j = s - 2
                            b = j // 2
                            act.wait_ge(t_psum, n * ITEMS + j + 1)
                            if b >= 2:
                                act.wait_ge(v_psum, n * HB + b - 1)
                            act.copy(probt[:, b % 2, :, j % 2, :],
                                     ps[0:LC, T_BANK, 0:LCN * S].rearrange("p (c s) -> p c s", c=LCN)
                                     ).then_inc(t_out, 1)
                        if s == NARROW[-1]:
                            rank_out(n, 1)
                        if s == ABSORB:
                            qk_high(n, 1)
                        if s in AHEAD and not last:
                            high(n + 1, AHEAD.index(s))

                high(0, 0)
                high(0, 1)
                with act.Fori(0, PAIRS // 2 - 1) as i:
                    for par in range(2):
                        pair(i * 2 + par, early=par == 0)
                pair(PAIRS - 2)
                pair(PAIRS - 1, last=True, early=False)

            @block.vector
            def _(dve):
                def low(n, u):
                    dve.wait_ge(a_high, n * UNITS + u + 1)
                    dve.tensor_tensor(ql[:, u % 2, :], ps[:, u % 2, 0:NT], qh[:, u % 2, :].bitcast(F32),
                                      ALU.subtract).then_inc(a_low, 1)

                def rope(n, u, c):
                    run, h = u // 2, u % 2
                    k = u * CB + c
                    if u == 2 and c < CB - 1:
                        dve.wait_ge(c_block, n * (CB - 1) + c + 1)
                    elif u == 2:
                        dve.wait_ge(c_psum, n * (UNITS // 2) + 1)
                    dve.wait_ge(b_psum, n * UNITS * CB + k + 1)
                    for v in range(2):
                        dve.tensor_tensor(
                            roped[:, h, v, c, :].rearrange("p (b s) -> p b s", b=GB),
                            ps[:, B_BANKS[k % 2], 0:NT].rearrange("p (b s) -> p b s", b=GB),
                            trig[:, v, c, :].unsqueeze(1).to_broadcast([128, GB, S]),
                            ALU.mult).then_inc(b_done, 1)

                def qk_low(n, run, h):
                    dve.wait_ge(k_high, n * UNITS + 2 * run + h + 1)
                    rs = slice(run * NT, (run + 1) * NT)
                    dve.tensor_tensor(kl[:, h, rs], ps[:, K_BANKS[run][h], 0:NT],
                                      kh[:, h, rs].bitcast(F32), ALU.subtract).then_inc(k_low, 1)

                def wout_low(n, h):
                    dve.wait_ge(m_high, n * 2 + h + 1)
                    dve.scalar_tensor_tensor(out=ml[:, h, :], in0=ps[:, 4 + h, :],
                                             scalar=core.gates[:, 0:1], in1=mh[:, h, :].bitcast(F32),
                                             op0=ALU.mult, op1=ALU.subtract).then_inc(m_low, 1)

                def pair(n, last=False):
                    rope(n, 0, 0)
                    rope(n, 0, 1)
                    rope(n, 0, 2)
                    low(n, 2)
                    rope(n, 1, 0)
                    rope(n, 1, 1)
                    rope(n, 1, 2)
                    low(n, 3)
                    for c in range(CB):
                        rope(n, 2, c)
                    qk_low(n, 0, 0)
                    qk_low(n, 0, 1)
                    rope(n, 3, 0)
                    for s in range(SLOTS):
                        if s < ITEMS:
                            dve.wait_ge(s_psum, n * ITEMS + s + 1)
                            dve.tensor_reduce(nmax[:, s % 4:s % 4 + 1], ps[0:S, s % 2, 0:L], AX.X, ALU.max,
                                              negate=True).then_inc(s_max, 1)
                        if 1 <= s < ITEMS + 1:
                            j = s - 1
                            dve.wait_ge(s_exp, n * ITEMS + j + 1)
                            dve.reciprocal(rsum[:, j % 4:j % 4 + 1], sums[:, j % 4:j % 4 + 1]).then_inc(s_rec, 1)
                            dve.wait_ge(s_rec, n * ITEMS + j + 1)
                            dve.tensor_scalar(prob[:, j % 4, 0:L], prob[:, j % 4, 0:L],
                                              rsum[:, j % 4:j % 4 + 1], None, ALU.mult).then_inc(s_norm, 1)
                        if s in WIDEN_LAST:
                            rope(n, 3, 1 + WIDEN_LAST.index(s))
                        if s in (MIX - 2, MIX - 1):
                            wout_low(n, s - MIX + 2)
                        if s in (ABSORB + 1, ABSORB + 2):
                            qk_low(n, 1, s - ABSORB - 1)
                        if s in range(MIX, MIX + ITEMS, 2):
                            b = (s - MIX) // 2
                            dve.wait_ge(v_high, n * HB + b + 1)
                            dve.tensor_tensor(cl[:, b % 2, :, :].rearrange("p h s -> p (h s)"),
                                              ps[:, V_BANK, 0:2 * S],
                                              ch[:, b % 2, :, :].rearrange("p h s -> p (h s)").bitcast(F32),
                                              ALU.subtract).then_inc(v_low, 1)
                        if s in range(OUT, OUT + ITEMS, 2):
                            b = (s - OUT) // 2
                            dve.wait_ge(o_psum, n * HB + b + 1)
                            x = core.x[:, b0 + b, :]
                            dve.tensor_tensor(x, x, ps[0:S, O_BANK, :], ALU.add).then_inc(o_add, 1)
                        if s in AHEAD and not last:
                            low(n + 1, AHEAD.index(s))

                low(0, 0)
                low(0, 1)
                with dve.Fori(0, PAIRS // 2 - 1) as i:
                    for par in range(2):
                        pair(i * 2 + par)
                pair(PAIRS - 2)
                pair(PAIRS - 1, last=True)


DI = 2048
IC = DI // 128
NC = DI // 512
ROUND = 12582912.0
W_COUNT = float(DI * D)


def quantised_ffn(core, w_ffn):
    nc, ps = core.nc, core.ps
    tag = "qf_"
    GATE, UP, DOWN = range(3)
    with ExitStack() as own:
        def sb(name, shape, dt=F32):
            return core.sbuf(tag + name, shape, dt, own)

        def sem(name):
            return core.sem(tag + name)

        raw = sb("raw_weights", [128, 2, KC * DI])
        wq = sb("sign_weights", [128, 3, KC * DI], BF16)
        xqt = sb("x_quant_t", [128, KC, B * S], BF16)
        wsum, wscale, winv = sb("w_abs_sums", [128, 3]), sb("w_scale", [128, 3]), sb("w_inverse", [128, 3])
        ones = sb("ones", [128, 128])
        identb = sb("identity_bf16", [128, 128], BF16)
        rnd = sb("rounder", [128, 1])
        xmax, xscale, xinv = sb("x_max", [S, B]), sb("x_scale", [S, B]), sb("x_inverse", [S, B])
        gscale, uscale = sb("gate_scale", [S, B]), sb("up_scale", [S, B])
        hmax, hscale, hinv = sb("h_max", [S, 2]), sb("h_scale", [S, 2]), sb("h_inverse", [S, 2])
        oscale = sb("out_scale", [S, 2])
        dscale = sb("down_scale", [128, 1])
        h = sb("hidden", [S, 2, DI])
        hq = sb("hidden_quant", [S, 2, DI], BF16)
        hqt = sb("hidden_quant_t", [128, 2, IC, S], BF16)
        xn = [h[:, i, 0:D] for i in range(2)]
        xq = [hq[:, i, 0:D] for i in range(2)]
        ns = NormSems(core, tag)
        loaded = [sem(f"w_loaded{i}") for i in range(3)]
        consts = sem("consts")
        w_abs, w_tot, w_inv, w_small = sem("w_abs"), sem("w_total"), sem("w_inv"), sem("w_small")
        w_up, w_clip, w_done = sem("w_scaled"), sem("w_clipped"), sem("w_done")
        n_done, n_max, n_small, n_mul, n_q = sem("normed"), sem("x_absmax"), sem("x_small"), sem("x_scaled"), sem("x_quant")
        x_t, x_done = sem("x_transposed"), sem("x_t_out")
        scales = sem("scales")

        def psb(t):
            return ps[:, t % 2, :].bitcast(BF16)[:, 0:KC * S].rearrange("p (k s) -> p k s", k=KC)

        with nc.Block() as block:
            @block.sync
            def _(sp):
                for m in range(3):
                    if m == 2:
                        sp.wait_ge(w_done, 1)
                    sp.dma_start(raw[:, m % 2, :], w_ffn[m]).then_inc(loaded[m], 16)

            @block.gpsimd
            def _(pool):
                pool.memset(ones[:], 1.0).then_inc(consts, 1)
                pool.memset(rnd[:], ROUND).then_inc(consts, 1)
                pool.tensor_copy(identb[:], core.ident[:]).then_inc(consts, 1)

            @block.scalar
            def _(act):
                norm_stats_act(act, core, ns, range(B))
                act.wait_ge(consts, 3)
                for m in range(2):
                    act.wait_ge(loaded[m], 16)
                    act.activation(wq[:, m, :], raw[:, m, :], ACT.Abs,
                                   accum_out=wsum[:, m:m + 1]).then_inc(w_abs, 1)
                for m in range(3):
                    act.wait_ge(w_inv, m + 1)
                    act.activation(raw[:, m % 2, :], raw[:, m % 2, :], ACT.Identity, bias=rnd[:, 0:1],
                                   scale=winv[:, m:m + 1]).then_inc(w_up, 1)
                    if m == 0:
                        act.wait_ge(loaded[2], 16)
                        act.activation(wq[:, 2, :], raw[:, 0, :], ACT.Abs,
                                       accum_out=wsum[:, 2:3]).then_inc(w_abs, 1)

            @block.vector
            def _(dve):
                norm_stats_dve(dve, core, ns, range(B))
                small = [0]

                def chain(ins):
                    small[0] += 1
                    ins.then_inc(w_small, 1)
                    dve.wait_ge(w_small, small[0])

                def inverse(m):
                    dve.wait_ge(w_tot, m + 1)
                    chain(dve.tensor_scalar(wscale[:, m:m + 1], ps[:, 5 + m, 0:1], 1.0 / W_COUNT, EPS,
                                            ALU.mult, ALU.add))
                    dve.reciprocal(winv[:, m:m + 1], wscale[:, m:m + 1]).then_inc(w_inv, 1)

                def quantise(m):
                    dve.wait_ge(w_up, m + 1)
                    dve.tensor_scalar(raw[:, m % 2, :], raw[:, m % 2, :], ROUND - 1.0, ROUND + 1.0,
                                      ALU.max, ALU.min).then_inc(w_clip, 1)
                    dve.wait_ge(w_clip, m + 1)
                    dve.tensor_scalar(wq[:, m, :], raw[:, m % 2, :], ROUND, None,
                                      ALU.subtract).then_inc(w_done, 1)

                inverse(0)
                inverse(1)
                quantise(0)
                for t in range(B):
                    k = t % 2
                    if t >= 2:
                        dve.wait_ge(n_mul, t - 1)
                    dve.tensor_scalar(xn[k], core.x[:, t, :], core.rstd[:, t:t + 1],
                                      core.nmr[:, t:t + 1], ALU.mult, ALU.add).then_inc(n_done, 1)
                    dve.wait_ge(n_done, t + 1)
                    dve.tensor_reduce(xmax[:, t:t + 1], xn[k], AX.X, ALU.max,
                                      apply_absolute_value=True).then_inc(n_max, 1)
                    dve.wait_ge(n_max, t + 1)
                    dve.tensor_scalar(xscale[:, t:t + 1], xmax[:, t:t + 1], 1.0 / 127.0, EPS,
                                      ALU.mult, ALU.add).then_inc(n_small, 1)
                    dve.wait_ge(n_small, 2 * t + 1)
                    dve.reciprocal(xinv[:, t:t + 1], xscale[:, t:t + 1]).then_inc(n_small, 1)
                    dve.wait_ge(n_small, 2 * t + 2)
                    dve.tensor_scalar(xn[k], xn[k], xinv[:, t:t + 1], ROUND, ALU.mult, ALU.add).then_inc(n_mul, 1)
                    dve.wait_ge(n_mul, t + 1)
                    if t >= 2:
                        dve.wait_ge(x_t, t - 1)
                    dve.tensor_scalar(xq[k], xn[k], ROUND, 127.0, ALU.subtract, ALU.min).then_inc(n_q, 1)
                    if t >= 1:
                        dve.wait_ge(x_t, t)
                        dve.tensor_copy(xqt[:, :, (t - 1) * S:t * S], psb(t - 1)).then_inc(x_done, 1)
                    if t == 4:
                        inverse(2)
                        quantise(1)
                    if t == 12:
                        quantise(2)
                dve.wait_ge(x_t, B)
                dve.tensor_copy(xqt[:, :, (B - 1) * S:], psb(B - 1)).then_inc(x_done, 1)
                dve.tensor_scalar(gscale[:], xscale[:], wscale[0:S, GATE:GATE + 1], None, ALU.mult).then_inc(scales, 1)
                dve.tensor_scalar(uscale[:], xscale[:], wscale[0:S, UP:UP + 1], None, ALU.mult).then_inc(scales, 1)
                dve.tensor_scalar(dscale[:], wscale[:, DOWN:DOWN + 1], core.gates[:, 2:3], None,
                                  ALU.mult).then_inc(scales, 1)

            @block.tensor
            def _(pe):
                pe.wait_ge(consts, 3)
                for m in range(2):
                    pe.wait_ge(w_abs, m + 1)
                    pe.matmul(ps[:, 5 + m, 0:1], ones[:], wsum[:, m:m + 1], start=True, stop=True).then_inc(w_tot, 1)
                for t in range(B):
                    pe.wait_ge(n_q, t + 1)
                    if t >= 2:
                        pe.wait_ge(x_done, t - 1)
                    for k in range(KC):
                        mm = pe.transpose(psb(t)[:, k, :], xq[t % 2][:, k * 128:(k + 1) * 128],
                                          identb[0:S, 0:S])
                    mm.then_inc(x_t, 1)
                    if t == 3:
                        pe.wait_ge(w_abs, 3)
                        pe.matmul(ps[:, 7, 0:1], ones[:], wsum[:, 2:3], start=True, stop=True).then_inc(w_tot, 1)

        gs, gs_ready = sb("gate_scale_of_tile", [S, 2]), sem("gate_scale_ready")
        g_psum, u_psum, g_out, u_out = sem("gate_psum"), sem("up_psum"), sem("gate_out"), sem("up_out")
        h_max, h_small, h_mul, h_q = sem("h_absmax"), sem("h_small"), sem("h_scaled"), sem("h_quant")
        t_psum, t_out = sem("h_t_psum"), sem("h_t_out")
        o_psum, o_add = sem("out_psum"), sem("out_added")

        def pst(half):
            return ps[:, 4 + half, :].bitcast(BF16)[:, 0:IC // 2 * S].rearrange("p (k s) -> p k s", k=IC // 2)

        with nc.Block() as block:
            @block.tensor
            def _(pe):
                def widen(t, first=False):
                    for c in range(NC):
                        for m, bank, psum, read in ((GATE, 0, g_psum, g_out), (UP, 2, u_psum, u_out)):
                            if c >= 2 or not first:
                                pe.wait_ge(read, t * NC + c - 1)
                            for k in range(KC):
                                mm = pe.matmul(ps[0:S, bank + c % 2, :], xqt[:, k, bass.ds(t * S, S)],
                                               wq[:, m, k * DI + c * 512:k * DI + (c + 1) * 512],
                                               start=(k == 0), stop=(k == KC - 1))
                            mm.then_inc(psum, 1)

                def narrow(t, par, first=False):
                    pe.wait_ge(h_q, t + 1)
                    for half in range(2):
                        if not first:
                            pe.wait_ge(t_out, t * 2 + half - 1)
                        for k in range(IC // 2):
                            i = half * (IC // 2) + k
                            mm = pe.transpose(pst(half)[:, k, :], hq[:, par, i * 128:(i + 1) * 128],
                                              identb[0:S, 0:S])
                        mm.then_inc(t_psum, 1)
                    pe.wait_ge(t_out, t * 2 + 2)
                    for i in range(IC):
                        mm = pe.matmul(ps[0:S, 6 + par, :], hqt[:, par, i, :], wq[:, DOWN, i * D:(i + 1) * D],
                                       start=(i == 0), stop=(i == IC - 1))
                    mm.then_inc(o_psum, 1)

                widen(0, True)
                widen(1)
                narrow(0, 0, True)
                with pe.Fori(0, B // 2 - 1) as i:
                    for par in range(2):
                        widen(i * 2 + par + 2)
                        narrow(i * 2 + par + 1, 1 - par)
                narrow(B - 1, 1)

            @block.scalar
            def _(act):
                def own_scale(t, par):
                    act.copy(gs[:, par:par + 1], gscale[:, bass.ds(t, 1)]).then_inc(gs_ready, 1)

                def widen(t, par, c):
                    act.wait_ge(gs_ready, t + 1)
                    act.wait_ge(g_psum, t * NC + c + 1)
                    act.activation(h[:, par, c * 512:(c + 1) * 512], ps[0:S, c % 2, :], ACT.Silu,
                                   scale=gs[:, par:par + 1]).then_inc(g_out, 1)

                def turn(t, par):
                    for half in range(2):
                        act.wait_ge(t_psum, t * 2 + half + 1)
                        act.copy(hqt[:, par, half * (IC // 2):(half + 1) * (IC // 2), :], pst(half)).then_inc(t_out, 1)

                def tile(t, par, last=False):
                    turn(t, par)
                    if not last:
                        own_scale(t + 2, par)
                        for c in range(NC):
                            widen(t + 2, par, c)

                for t in range(2):
                    own_scale(t, t)
                    for c in range(NC):
                        widen(t, t, c)
                with act.Fori(0, B // 2 - 1) as i:
                    for par in range(2):
                        tile(i * 2 + par, par)
                for t in (B - 2, B - 1):
                    tile(t, t % 2, True)

            @block.vector
            def _(dve):
                def widen(t, par):
                    for c in range(NC):
                        cs = slice(c * 512, (c + 1) * 512)
                        dve.wait_ge(u_psum, t * NC + c + 1)
                        dve.wait_ge(g_out, t * NC + c + 1)
                        dve.scalar_tensor_tensor(out=h[:, par, cs], in0=ps[0:S, 2 + c % 2, :],
                                                 scalar=uscale[:, bass.ds(t, 1)], in1=h[:, par, cs],
                                                 op0=ALU.mult, op1=ALU.mult).then_inc(u_out, 1)

                def quantise(t, par):
                    k = slice(par, par + 1)
                    dve.wait_ge(u_out, t * NC + NC)
                    dve.tensor_reduce(hmax[:, k], h[:, par, :], AX.X, ALU.max,
                                      apply_absolute_value=True).then_inc(h_max, 1)
                    dve.wait_ge(h_max, t + 1)
                    dve.tensor_scalar(hscale[:, k], hmax[:, k], 1.0 / 127.0, EPS,
                                      ALU.mult, ALU.add).then_inc(h_small, 1)
                    dve.wait_ge(h_small, t * 3 + 1)
                    dve.reciprocal(hinv[:, k], hscale[:, k]).then_inc(h_small, 1)
                    dve.tensor_scalar(oscale[:, k], hscale[:, k], dscale[0:S, 0:1], None,
                                      ALU.mult).then_inc(h_small, 1)
                    dve.wait_ge(h_small, t * 3 + 3)
                    dve.tensor_scalar(h[:, par, :], h[:, par, :], hinv[:, k], ROUND,
                                      ALU.mult, ALU.add).then_inc(h_mul, 1)
                    dve.wait_ge(h_mul, t + 1)
                    dve.tensor_scalar(hq[:, par, :], h[:, par, :], ROUND, 127.0,
                                      ALU.subtract, ALU.min).then_inc(h_q, 1)

                def add(t, par):
                    dve.wait_ge(o_psum, t + 1)
                    x = core.x[:, bass.ds(t, 1), :].rearrange("p t d -> p (t d)")
                    dve.scalar_tensor_tensor(out=x, in0=ps[0:S, 6 + par, :], scalar=oscale[:, par:par + 1],
                                             in1=x, op0=ALU.mult, op1=ALU.add).then_inc(o_add, 1)

                widen(0, 0)
                quantise(0, 0)
                widen(1, 1)
                quantise(1, 1)
                with dve.Fori(0, B // 2 - 1) as i:
                    for par in range(2):
                        t = i * 2 + par
                        widen(t + 2, par)
                        add(t, par)
                        quantise(t + 2, par)
                add(B - 2, 0)
                add(B - 1, 1)


H1 = 16
HD = D // H1
HPB = 128 // HD
A_Q, A_O, A_K, A_V = 0, KC * D, 2 * KC * D, 2 * KC * D + D
A_ALL = A_V + D
FAR = -3.0e38


def causal_attention(core, ctx_in, w_att):
    nc, ps = core.nc, core.ps
    tag = "ca_"
    with ExitStack() as own:
        def sb(name, shape, dt=F32):
            return core.sbuf(tag + name, shape, dt, own)

        def sem(name):
            return core.sem(tag + name)

        w = sb("weights", [128, A_ALL])
        wqh, wql = sb("wq_high", [128, KC, D], F32R), sb("wq_low", [128, KC, D], F32R)
        woh, wol = sb("wo_high", [128, KC, D], F32R), sb("wo_low", [128, KC, D], F32R)
        lat = sb("latents", [S, B, DC])
        xn = sb("xn", [S, 2, D])
        xth, xtl = sb("xn_t_high", [128, KC, NT], F32R), sb("xn_t_low", [128, KC, NT], F32R)
        latt = sb("latents_t", [DC, GB, S])
        lats = sb("latents_now", [S, GB, DC])
        qt = sb("q_t", [128, KC, GB, S])
        kt = sb("k_t_by_head", [128, GB, KC, HPB, S])
        v = sb("values", [S, 2, D])
        p = sb("probs", [S, 4, HPB, S])
        pt = sb("probs_t", [S, 2, KC, HPB, S])
        oh, ol = sb("heads_high", [128, 2, KC, S], F32R), sb("heads_low", [128, 2, KC, S], F32R)
        mask = sb("mask", [S, S])
        mx, sm, rs = sb("maxima", [S, 4, HPB]), sb("sums", [S, 4, HPB]), sb("rsums", [S, 4, HPB])
        ns = NormSems(core, tag)
        w_in, l_in, mask_zero, consts = sem("weights_in"), sem("latents_in"), sem("mask_zero"), sem("consts")
        w_high, w_low = sem("weights_high"), sem("weights_low")
        normed, x_t, x_high, x_low = sem("normed"), sem("x_transposed"), sem("x_high"), sem("x_low")
        l_now, l_t, l_out = sem("latents_moved"), sem("latents_transposed"), sem("latents_t_out")
        q_psum, q_out, k_psum, k_out = sem("q_psum"), sem("q_out"), sem("k_psum"), sem("k_out")
        v_psum, v_out = sem("v_psum"), sem("v_out")
        s_psum, s_mask, s_max, s_sub = sem("scores"), sem("scores_masked"), sem("scores_max"), sem("scores_less_max")
        s_exp, s_sum, s_rec, s_norm = sem("scores_exp"), sem("exp_sum"), sem("rsum"), sem("probs_normed")
        t_psum, t_out = sem("probs_t_psum"), sem("probs_t_out")
        m_psum, m_high, m_low = sem("heads_psum"), sem("heads_high"), sem("heads_low")
        o_psum, o_add = sem("out_psum"), sem("out_added")
        ITEMS = GB * KC
        SLOTS = ITEMS + 6
        PV_AT, OUT_AT = 7, 9

        with nc.Block() as block:
            @block.sync
            def _(sp):
                sp.dma_start(w[:], w_att).then_inc(w_in, 16)
                sp.dma_start(lat[:], ctx_in[:, 0:S, :].rearrange("b p d -> p b d")).then_inc(l_in, 16)

            @block.gpsimd
            def _(pool):
                pool.memset(kt[:], 0.0).then_inc(consts, 1)
                pool.memset(mask[:], 0.0).then_inc(mask_zero, 1)
                pool.wait_ge(mask_zero, 1)
                pool.affine_select(out=mask[:], in_=mask[:], compare_op=ALU.is_ge, fill=FAR, base=0,
                                   pattern=[[-1, S]], channel_multiplier=1).then_inc(consts, 1)

            @block.scalar
            def _(act):
                norm_stats_act(act, core, ns, range(B))

            @block.vector
            def _(dve):
                norm_stats_dve(dve, core, ns, range(B))
                dve.wait_ge(w_in, 16)
                for k, (high, low, at) in enumerate(((wqh, wql, A_Q), (woh, wol, A_O))):
                    hv, lv = (a[:].rearrange("p k d -> p (k d)") for a in (high, low))
                    dve.tensor_copy(hv, w[:, at:at + KC * D]).then_inc(w_high, 1)
                    dve.wait_ge(w_high, k + 1)
                    dve.tensor_tensor(lv, w[:, at:at + KC * D], hv.bitcast(F32), ALU.subtract).then_inc(w_low, 1)
                dve.wait_ge(l_in, 16)

        with nc.Block() as block:
            @block.tensor
            def _(pe):
                def scores(g, j):
                    b, c = j // KC, j % KC
                    if j >= 2:
                        pe.wait_ge(s_mask, g * ITEMS + j - 1)
                    pe.matmul(ps[0:S, j % 2, 0:NT], qt[:, c, b, :],
                              kt[:, b, c, :, :].rearrange("p h s -> p (h s)"),
                              start=True, stop=True).then_inc(s_psum, 1)

                def values(g, b):
                    if b >= 1:
                        pe.wait_ge(v_out, g * GB + b)
                    pe.matmul(ps[0:S, 4, :], latt[:, b, :], w[:, A_V:A_ALL],
                              start=True, stop=True).then_inc(v_psum, 1)

                def turn(g, j):
                    pe.wait_ge(s_norm, g * ITEMS + j + 1)
                    if j >= 2:
                        pe.wait_ge(t_out, g * ITEMS + j - 1)
                    for h in range(HPB):
                        mm = pe.transpose(ps[0:S, 2 + j % 2, h * S:(h + 1) * S], p[:, j % 4, h, :],
                                          core.ident[0:S, 0:S])
                    mm.then_inc(t_psum, 1)

                def mix(g, b):
                    pe.wait_ge(t_out, g * ITEMS + (b + 1) * KC)
                    pe.wait_ge(v_out, g * GB + b + 1)
                    for c in range(KC):
                        for h in range(HPB):
                            at = c * 128 + h * HD
                            mm = pe.matmul(ps[h * HD:(h + 1) * HD, 5, c * S:(c + 1) * S],
                                           v[:, b % 2, at:at + HD], pt[:, b % 2, c, h, :],
                                           start=True, stop=True)
                    mm.then_inc(m_psum, 1)

                def out(g, b):
                    pe.wait_ge(m_low, g * GB + b + 1)
                    if b >= 2:
                        pe.wait_ge(o_add, g * GB + b - 1)
                    for c in range(KC):
                        for k, (a, m) in enumerate(((oh, woh), (oh, wol), (ol, woh))):
                            mm = pe.matmul(ps[0:S, 6 + b % 2, :], a[:, b % 2, c, :], m[:, c, :],
                                           start=(c == 0 and k == 0), stop=(c == KC - 1 and k == 2))
                    mm.then_inc(o_psum, 1)

                with pe.Fori(0, B // GB) as g:
                    for t in range(GB):
                        pe.wait_ge(normed, g * GB + t + 1)
                        if t >= 2:
                            pe.wait_ge(x_low, g * GB + t - 1)
                        for k in range(KC):
                            mm = pe.transpose(ps[:, t % 2, k * S:(k + 1) * S], xn[:, t % 2, k * 128:(k + 1) * 128],
                                              core.ident[0:S, 0:S])
                        mm.then_inc(x_t, 1)
                    pe.wait_ge(l_now, g + 1)
                    for t in range(GB):
                        mm = pe.transpose(ps[:, 2, t * S:(t + 1) * S], lats[:, t, :], core.ident[0:S, 0:S])
                    mm.then_inc(l_t, 1)
                    pe.wait_ge(x_low, g * GB + GB)
                    for c in range(KC):
                        if c >= 2:
                            pe.wait_ge(q_out, g * KC + c - 1)
                        for k in range(KC):
                            for i, (a, x) in enumerate(((wqh, xth), (wqh, xtl), (wql, xth))):
                                mm = pe.matmul(ps[:, 4 + c % 2, 0:NT], a[:, k, c * 128:(c + 1) * 128], x[:, k, :],
                                               start=(k == 0 and i == 0), stop=(k == KC - 1 and i == 2))
                        mm.then_inc(q_psum, 1)
                    pe.wait_ge(l_out, g + 1)
                    for c in range(KC):
                        if c >= 2:
                            pe.wait_ge(k_out, g * KC * HPB + (c - 1) * HPB)
                        pe.matmul(ps[:, c % 2, 0:NT], w[:, A_K + c * 128:A_K + (c + 1) * 128],
                                  latt[:].rearrange("p b s -> p (b s)"), start=True, stop=True).then_inc(k_psum, 1)
                    pe.wait_ge(q_out, g * KC + KC)
                    pe.wait_ge(k_out, (g + 1) * KC * HPB)
                    for s in range(SLOTS):
                        if s < ITEMS:
                            scores(g, s)
                            if s % KC == 0:
                                values(g, s // KC)
                        if 3 <= s < ITEMS + 3:
                            turn(g, s - 3)
                        if s >= PV_AT and (s - PV_AT) % KC == 0:
                            mix(g, (s - PV_AT) // KC)
                        if s >= OUT_AT and (s - OUT_AT) % KC == 0:
                            out(g, (s - OUT_AT) // KC)

            @block.scalar
            def _(act):
                with act.Fori(0, B // GB) as g:
                    for t in range(GB):
                        act.wait_ge(x_t, g * GB + t + 1)
                        act.copy(xth[:, :, t * S:(t + 1) * S],
                                 ps[:, t % 2, 0:KC * S].rearrange("p (k s) -> p k s", k=KC)).then_inc(x_high, 1)
                    act.wait_ge(l_t, g + 1)
                    act.copy(latt[:].rearrange("p b s -> p (b s)"), ps[:, 2, 0:GB * S]).then_inc(l_out, 1)
                    for c in range(KC):
                        act.wait_ge(q_psum, g * KC + c + 1)
                        act.activation(qt[:, c].rearrange("p b s -> p (b s)"), ps[:, 4 + c % 2, 0:NT], ACT.Copy,
                                       scale=float(HD) ** -0.5).then_inc(q_out, 1)
                    for c in range(KC):
                        act.wait_ge(k_psum, g * KC + c + 1)
                        for h in range(HPB):
                            hp = slice(h * HD, (h + 1) * HD)
                            act.copy(kt[hp, :, c, h, :],
                                     ps[hp, c % 2, 0:NT].rearrange("p (b s) -> p b s", b=GB)).then_inc(k_out, 1)
                    for s in range(SLOTS):
                        if 3 <= s < ITEMS + 3:
                            j = s - 3
                            b = j // KC
                            act.wait_ge(t_psum, g * ITEMS + j + 1)
                            if b >= 2:
                                act.wait_ge(m_psum, g * GB + b - 1)
                            act.copy(pt[:, b % 2, j % KC].rearrange("p h s -> p (h s)"),
                                     ps[0:S, 2 + j % 2, 0:NT]).then_inc(t_out, 1)
                        if s < ITEMS:
                            act.wait_ge(s_sub, g * ITEMS + s + 1)
                            ps_ = p[:, s % 4].rearrange("p h s -> p (h s)")
                            act.activation(ps_, ps_, ACT.Exp).then_inc(s_exp, 1)
                        if s >= PV_AT and (s - PV_AT) % KC == 0:
                            b = (s - PV_AT) // KC
                            act.wait_ge(m_psum, g * GB + b + 1)
                            if b >= 2:
                                act.wait_ge(o_psum, g * GB + b - 1)
                            act.activation(oh[:, b % 2].rearrange("p c s -> p (c s)"), ps[:, 5, 0:KC * S],
                                           ACT.Copy, scale=core.gates[:, 1:2]).then_inc(m_high, 1)

            @block.gpsimd
            def _(pool):
                with pool.Fori(0, B // GB) as g:
                    for s in range(ITEMS + 2):
                        if s >= 2:
                            k = (s - 2) % 4
                            pool.wait_ge(s_rec, g * ITEMS + s - 1)
                            pool.tensor_tensor(p[:, k], p[:, k], rs[:, k].unsqueeze(2).to_broadcast([S, HPB, S]),
                                               ALU.mult).then_inc(s_norm, 1)
                        if s < ITEMS:
                            k = s % 4
                            pool.wait_ge(s_max, g * ITEMS + s + 1)
                            pool.tensor_tensor(p[:, k], p[:, k], mx[:, k].unsqueeze(2).to_broadcast([S, HPB, S]),
                                               ALU.subtract).then_inc(s_sub, 1)

            @block.vector
            def _(dve):
                with dve.Fori(0, B // GB) as g:
                    for t in range(GB):
                        if t >= 2:
                            dve.wait_ge(x_t, g * GB + t - 1)
                        at = g * GB + t
                        dve.tensor_scalar(xn[:, t % 2, :], core.x[:, bass.ds(at, 1), :].rearrange("p t d -> p (t d)"),
                                          core.rstd[:, bass.ds(at, 1)], core.nmr[:, bass.ds(at, 1)],
                                          ALU.mult, ALU.add).then_inc(normed, 1)
                        if t == 0:
                            dve.tensor_copy(lats[:], lat[:, bass.ds(g * GB, GB), :]).then_inc(l_now, 1)
                        if t >= 1:
                            dve.wait_ge(x_high, g * GB + t)
                            dve.tensor_tensor(xtl[:, :, (t - 1) * S:t * S],
                                              ps[:, (t - 1) % 2, 0:KC * S].rearrange("p (k s) -> p k s", k=KC),
                                              xth[:, :, (t - 1) * S:t * S].bitcast(F32), ALU.subtract).then_inc(x_low, 1)
                    dve.wait_ge(x_high, g * GB + GB)
                    dve.tensor_tensor(xtl[:, :, (GB - 1) * S:],
                                      ps[:, (GB - 1) % 2, 0:KC * S].rearrange("p (k s) -> p k s", k=KC),
                                      xth[:, :, (GB - 1) * S:].bitcast(F32), ALU.subtract).then_inc(x_low, 1)
                    for s in range(SLOTS):
                        if 2 <= s < ITEMS + 2:
                            j = s - 2
                            k = j % 4
                            dve.wait_ge(s_exp, g * ITEMS + j + 1)
                            dve.tensor_reduce(sm[:, k], p[:, k], AX.X, ALU.add).then_inc(s_sum, 1)
                            dve.wait_ge(s_sum, g * ITEMS + j + 1)
                            dve.reciprocal(rs[:, k], sm[:, k]).then_inc(s_rec, 1)
                        if s < ITEMS:
                            k = s % 4
                            dve.wait_ge(s_psum, g * ITEMS + s + 1)
                            dve.tensor_tensor(p[:, k], ps[0:S, s % 2, 0:NT].rearrange("p (h s) -> p h s", h=HPB),
                                              mask[:].unsqueeze(1).to_broadcast([S, HPB, S]),
                                              ALU.add).then_inc(s_mask, 1)
                            dve.wait_ge(s_mask, g * ITEMS + s + 1)
                            dve.tensor_reduce(mx[:, k], p[:, k], AX.X, ALU.max).then_inc(s_max, 1)
                            if s % KC == 0:
                                b = s // KC
                                dve.wait_ge(v_psum, g * GB + b + 1)
                                dve.tensor_copy(v[:, b % 2, :], ps[0:S, 4, :]).then_inc(v_out, 1)
                        if s >= PV_AT and (s - PV_AT) % KC == 0:
                            b = (s - PV_AT) // KC
                            dve.wait_ge(m_high, g * GB + b + 1)
                            dve.scalar_tensor_tensor(out=ol[:, b % 2].rearrange("p c s -> p (c s)"),
                                                     in0=ps[:, 5, 0:KC * S], scalar=core.gates[:, 1:2],
                                                     in1=oh[:, b % 2].rearrange("p c s -> p (c s)").bitcast(F32),
                                                     op0=ALU.mult, op1=ALU.subtract).then_inc(m_low, 1)
                        if s >= OUT_AT and (s - OUT_AT) % KC == 0:
                            b = (s - OUT_AT) // KC
                            dve.wait_ge(o_psum, g * GB + b + 1)
                            x = core.x[:, bass.ds(g * GB + b, 1), :].rearrange("p t d -> p (t d)")
                            dve.tensor_tensor(x, x, ps[0:S, 6 + b % 2, :], ALU.add).then_inc(o_add, 1)


E = 7
EA = E + 1
MATS = 3
UP, GATE, DOWN = range(MATS)


def expert_ffn(core, w_exp, b_exp, b_down, w_router, b_router, order):
    nc, ps = core.nc, core.ps
    tag = "ex_"
    with ExitStack() as own:
        def sb(name, shape, dt=F32):
            return core.sbuf(tag + name, shape, dt, own)

        def sem(name):
            return core.sem(tag + name)

        xth, xtl = sb("xn_t_high", [128, KC, B * S], F32R), sb("xn_t_low", [128, KC, B * S], F32R)
        raw = sb("raw_weights", [128, MATS, KC * D])
        wh, wl = sb("weights_high", [128, MATS, KC * D], F32R), sb("weights_low", [128, MATS, KC * D], F32R)
        bias, bias_now = sb("biases", [128, EA, 2, KC]), sb("biases_now", [128, 2, KC])
        pg = sb("gated_probs", [S, B, EA])
        uh, ul = sb("u_high", [128, KC, NT], F32R), sb("u_low", [128, KC, NT], F32R)
        u = sb("u", [128, KC, NT])
        sg, gm = sb("silu_gate", [128, 2, NT]), sb("g", [128, 2, NT])
        gh, gl = sb("g_high", [128, KC, NT], F32R), sb("g_low", [128, KC, NT], F32R)
        flat = u[:].rearrange("p k n -> p (k n)")
        xn = [flat[0:S, i * D:(i + 1) * D] for i in range(2)]
        sgf, gmf = sg[:].rearrange("p k n -> p (k n)"), gm[:].rearrange("p k n -> p (k n)")
        bd = gmf[0:EA, 0:D]
        pgt = flat[0:EA, 0:B * S].rearrange("p (t s) -> p t s", t=B)
        wr = sgf[:, 0:KC * EA].rearrange("p (k e) -> p k e", k=KC)
        wrh, wrl = sb("router_high", [128, KC, EA], F32R), sb("router_low", [128, KC, EA], F32R)
        br = sb("router_bias", [S, 2, E])
        seq = sb("order", [S, E])
        logit, biased = sb("logits", [S, B, E]), sb("biased", [S, B, E])
        one, two, hit = sb("first", [S, B, E]), sb("second", [S, B, E]), sb("hit", [S, B, E])
        top = sb("top", [S, B])
        ns = NormSems(core, tag)
        w_in = [sem(f"weights_in{m}") for m in range(MATS)]
        small_in = sem("small_in")
        r_split = sem("router_split")
        normed, x_t, x_high, x_low = sem("normed"), sem("x_transposed"), sem("x_high"), sem("x_low")
        r_psum, step_done, d_exp, r_exp = sem("router_psum"), sem("router_step"), sem("less_max"), sem("router_exp")
        pg_done, pg_t, pg_out, b_psum, b_add = sem("probs"), sem("probs_turned"), sem("probs_t_out"), sem("bias_psum"), sem("bias_added")
        w_high, w_low = sem("weights_high"), sem("weights_low")
        bias_ready = sem("bias_ready")
        u_psum, u_high, u_low, u_sum = sem("u_psum"), sem("u_high"), sem("u_low"), sem("u_sum")
        g_psum, g_silu, g_mul, g_high, g_low = sem("g_psum"), sem("g_silu"), sem("g_mul"), sem("g_high"), sem("g_low")
        o_psum, o_add = sem("out_psum"), sem("out_added")

        def load(sp, e, m):
            sp.dma_start(raw[:, m, :], w_exp[e, m]).then_inc(w_in[m], 16)

        with nc.Block() as block:
            @block.sync
            def _(sp):
                for dst, src in ((wr, w_router), (bias[:], b_exp), (bd, b_down),
                                 (br[:].rearrange("p a e -> p (a e)"), b_router.rearrange("(o a) e -> o (a e)", o=1).to_broadcast([S, 2 * E])),
                                 (seq[:], order.rearrange("(o e) -> o e", o=1).to_broadcast([S, E]))):
                    sp.dma_start(dst, src).then_inc(small_in, 16)
                for m in range(MATS):
                    load(sp, 0, m)

            @block.scalar
            def _(act):
                norm_stats_act(act, core, ns, range(B))
                for t in range(B):
                    act.wait_ge(x_t, t + 1)
                    act.copy(xth[:, :, t * S:(t + 1) * S],
                             ps[:, t % 2, 0:KC * S].rearrange("p (k s) -> p k s", k=KC)).then_inc(x_high, 1)
                act.wait_ge(d_exp, 1)
                act.activation(hit[:], hit[:], ACT.Exp).then_inc(r_exp, 1)
                for k in range(4):
                    act.wait_ge(pg_t, k + 1)
                    act.copy(pgt[:, 4 * k:4 * k + 4, :].rearrange("p t s -> p (t s)"),
                             ps[0:EA, k, 0:4 * S]).then_inc(pg_out, 1)

            @block.vector
            def _(dve):
                norm_stats_dve(dve, core, ns, range(B))
                for t in range(B):
                    if t >= 2:
                        dve.wait_ge(x_t, t - 1)
                    dve.tensor_scalar(xn[t % 2], core.x[:, t, :], core.rstd[:, t:t + 1],
                                      core.nmr[:, t:t + 1], ALU.mult, ALU.add).then_inc(normed, 1)
                    if t >= 1:
                        dve.wait_ge(x_high, t)
                        dve.tensor_tensor(xtl[:, :, (t - 1) * S:t * S],
                                          ps[:, (t - 1) % 2, 0:KC * S].rearrange("p (k s) -> p k s", k=KC),
                                          xth[:, :, (t - 1) * S:t * S].bitcast(F32), ALU.subtract).then_inc(x_low, 1)
                    if t == 1:
                        dve.wait_ge(small_in, 80)
                        dve.tensor_copy(wrh[:], wr).then_inc(r_split, 1)
                        dve.wait_ge(r_split, 1)
                        dve.tensor_tensor(wrl[:], wr, wrh[:].bitcast(F32), ALU.subtract).then_inc(r_split, 1)
                dve.wait_ge(x_high, B)
                dve.tensor_tensor(xtl[:, :, (B - 1) * S:],
                                  ps[:, (B - 1) % 2, 0:KC * S].rearrange("p (k s) -> p k s", k=KC),
                                  xth[:, :, (B - 1) * S:].bitcast(F32), ALU.subtract).then_inc(x_low, 1)
                dve.wait_ge(r_psum, B)
                done = [0]

                def step(ins):
                    done[0] += 1
                    ins.then_inc(step_done, 1)
                    dve.wait_ge(step_done, done[0])

                wide = [S, B, E]
                tops = top[:].unsqueeze(2).to_broadcast(wide)
                seqs = seq[:].unsqueeze(1).to_broadcast(wide)
                step(dve.tensor_tensor(logit[:], ps[0:S, 2, 0:B * EA].rearrange("p (t e) -> p t e", t=B)[:, :, 0:E],
                                       br[:, 0, :].unsqueeze(1).to_broadcast(wide), ALU.add))
                step(dve.tensor_tensor(biased[:], logit[:], br[:, 1, :].unsqueeze(1).to_broadcast(wide), ALU.add))
                for which in (one, two):
                    step(dve.tensor_reduce(top[:], biased[:], AX.X, ALU.max))
                    step(dve.tensor_tensor(hit[:], biased[:], tops, ALU.is_equal))
                    step(dve.tensor_tensor(hit[:], hit[:], seqs, ALU.mult))
                    step(dve.tensor_reduce(top[:], hit[:], AX.X, ALU.max))
                    step(dve.tensor_tensor(which[:], hit[:], tops, ALU.is_equal))
                    step(dve.scalar_tensor_tensor(out=biased[:], in0=which[:], scalar=FAR, in1=biased[:],
                                                  op0=ALU.mult, op1=ALU.add))
                step(dve.tensor_tensor(one[:], one[:], two[:], ALU.add))
                step(dve.tensor_scalar(one[:], one[:], -FAR, FAR, ALU.mult, ALU.add))
                step(dve.tensor_tensor(logit[:], logit[:], one[:], ALU.add))
                step(dve.tensor_reduce(top[:], logit[:], AX.X, ALU.max))
                dve.tensor_tensor(hit[:], logit[:], tops, ALU.subtract).then_inc(d_exp, 1)
                dve.wait_ge(r_exp, 1)
                step(dve.tensor_reduce(top[:], hit[:], AX.X, ALU.add))
                step(dve.reciprocal(top[:], top[:]))
                step(dve.tensor_scalar(top[:], top[:], core.gates[0:S, 3:4], None, ALU.mult))
                dve.wait_ge(pg_done, 1)
                dve.tensor_tensor(pg[:, :, 0:E], hit[:], tops, ALU.mult).then_inc(pg_done, 1)
                dve.tensor_scalar(pg[:, :, E:EA], pg[:, :, E:EA], core.gates[0:S, 3:4], None,
                                  ALU.mult).then_inc(pg_done, 1)
                for t in range(B):
                    dve.wait_ge(b_psum, t + 1)
                    dve.tensor_tensor(core.x[:, t, :], core.x[:, t, :], ps[0:S, 4 + t % 4, :],
                                      ALU.add).then_inc(b_add, 1)

            @block.gpsimd
            def _(pool):
                pool.memset(pg[:], 1.0).then_inc(pg_done, 1)

            @block.tensor
            def _(pe):
                for t in range(B):
                    pe.wait_ge(normed, t + 1)
                    if t >= 2:
                        pe.wait_ge(x_low, t - 1)
                    for k in range(KC):
                        mm = pe.transpose(ps[:, t % 2, k * S:(k + 1) * S], xn[t % 2][:, k * 128:(k + 1) * 128],
                                          core.ident[0:S, 0:S])
                    mm.then_inc(x_t, 1)
                pe.wait_ge(r_split, 2)
                pe.wait_ge(x_low, B)
                for t in range(B):
                    for k in range(KC):
                        for i, (a, m) in enumerate(((xth, wrh), (xth, wrl), (xtl, wrh))):
                            mm = pe.matmul(ps[0:S, 2, t * EA:(t + 1) * EA], a[:, k, t * S:(t + 1) * S], m[:, k, :],
                                           start=(k == 0 and i == 0), stop=(k == KC - 1 and i == 2))
                    mm.then_inc(r_psum, 1)
                pe.wait_ge(pg_done, 3)
                for t in range(B):
                    mm = pe.transpose(ps[0:EA, t // 4, t % 4 * S:(t % 4 + 1) * S], pg[:, t, :],
                                      core.ident[0:S, 0:S])
                    if t % 4 == 3:
                        mm.then_inc(pg_t, 1)
                for t in range(B):
                    pe.wait_ge(pg_out, t // 4 + 1)
                    if t >= 4:
                        pe.wait_ge(b_add, t - 3)
                    pe.matmul(ps[0:S, 4 + t % 4, :], pgt[:, t, :], bd, start=True, stop=True).then_inc(b_psum, 1)

        RUNS = B // GB
        U = RUNS * KC

        def mat(w, m):
            return w[:, m, :].rearrange("p (k d) -> p k d", k=KC)

        with nc.Block() as block:
            @block.sync
            def _(sp):
                with sp.Fori(1, EA) as e:
                    for m in range(MATS):
                        sp.wait_ge(w_low, (e - 1) * MATS + m + 1)
                        load(sp, e, m)

            @block.tensor
            def _(pe):
                passes = ((0, 0), (0, 1), (1, 0))
                with pe.Fori(0, EA) as e:
                    for r in range(RUNS):
                        base = e * U + r * KC
                        if r == 0:
                            pe.wait_ge(w_low, e * MATS + UP + 1)
                        for c in range(KC):
                            if c >= 2:
                                pe.wait_ge(u_low, base + c - 1)
                            for k in range(KC):
                                for i, (a, x) in enumerate(passes):
                                    mm = pe.matmul(ps[:, c % 2, 0:NT],
                                                   mat((wh, wl)[a], UP)[:, k, c * 128:(c + 1) * 128],
                                                   (xth, xtl)[x][:, k, r * NT:(r + 1) * NT],
                                                   start=(k == 0 and i == 0), stop=(k == KC - 1 and i == 2))
                            mm.then_inc(u_psum, 1)
                        if r == 0:
                            pe.wait_ge(w_low, e * MATS + GATE + 1)
                        for c in range(KC):
                            if c >= 2:
                                pe.wait_ge(g_silu, base + c - 1)
                            for k in range(KC):
                                if c == 0:
                                    pe.wait_ge(u_low, base + k + 1)
                                for i, (a, x) in enumerate(passes):
                                    mm = pe.matmul(ps[:, 2 + c % 2, 0:NT],
                                                   mat((wh, wl)[a], GATE)[:, k, c * 128:(c + 1) * 128],
                                                   (uh, ul)[x][:, k, :],
                                                   start=(k == 0 and i == 0), stop=(k == KC - 1 and i == 2))
                            mm.then_inc(g_psum, 1)
                        if r == 0:
                            pe.wait_ge(w_low, e * MATS + DOWN + 1)
                        for t in range(GB):
                            for k in range(KC):
                                if t == 0:
                                    pe.wait_ge(g_low, base + k + 1)
                                for i, (a, x) in enumerate(passes):
                                    mm = pe.matmul(ps[0:S, 4 + t, :], (gh, gl)[x][:, k, t * S:(t + 1) * S],
                                                   mat((wh, wl)[a], DOWN)[:, k, :],
                                                   start=(k == 0 and i == 0), stop=(k == KC - 1 and i == 2))
                            mm.then_inc(o_psum, 1)

            @block.scalar
            def _(act):
                def high(e, m):
                    act.wait_ge(w_in[m], (e + 1) * 16)
                    act.copy(wh[:, m, :], raw[:, m, :]).then_inc(w_high, 1)

                def expert(e, last=False):
                    for r in range(RUNS):
                        base = e * U + r * KC
                        if r == 0:
                            act.wait_ge(bias_ready, e + 1)
                        for c in range(KC):
                            act.wait_ge(u_psum, base + c + 1)
                            act.activation(uh[:, c, :], ps[:, c % 2, 0:NT], ACT.Identity,
                                           bias=bias_now[:, UP, c:c + 1]).then_inc(u_high, 1)
                        if r == 0:
                            high(e, DOWN)
                        if r == RUNS - 1 and not last:
                            high(e + 1, UP)
                        for c in range(KC + 1):
                            if c < KC:
                                act.wait_ge(g_psum, base + c + 1)
                                if c >= 2:
                                    act.wait_ge(g_mul, base + c - 1)
                                act.activation(sg[:, c % 2, :], ps[:, 2 + c % 2, 0:NT], ACT.Silu,
                                               bias=bias_now[:, GATE, c:c + 1]).then_inc(g_silu, 1)
                            if c >= 1:
                                act.wait_ge(g_mul, base + c)
                                act.copy(gh[:, c - 1, :], gm[:, (c - 1) % 2, :]).then_inc(g_high, 1)
                        if r == RUNS - 1 and not last:
                            high(e + 1, GATE)

                high(0, UP)
                high(0, GATE)
                with act.Fori(0, EA - 1) as e:
                    expert(e)
                expert(EA - 1, True)

            @block.gpsimd
            def _(pool):
                with pool.Fori(0, EA) as e:
                    for r in range(RUNS):
                        base = e * U + r * KC
                        for c in range(KC):
                            pool.wait_ge(u_low, base + c + 1)
                            pool.tensor_tensor(u[:, c, :], uh[:, c, :].bitcast(F32), ul[:, c, :].bitcast(F32),
                                               ALU.add).then_inc(u_sum, 1)
                        for c in range(KC):
                            pool.wait_ge(g_high, base + c + 1)
                            pool.tensor_tensor(gl[:, c, :], gm[:, c % 2, :], gh[:, c, :].bitcast(F32),
                                               ALU.subtract).then_inc(g_low, 1)

            @block.vector
            def _(dve):
                def low(e, m):
                    dve.wait_ge(w_high, e * MATS + m + 1)
                    dve.tensor_tensor(wl[:, m, :], raw[:, m, :], wh[:, m, :].bitcast(F32),
                                      ALU.subtract).then_inc(w_low, 1)

                def expert(e, last=False):
                    dve.tensor_copy(bias_now[:].rearrange("p a c -> p (a c)"),
                                    bias[:, bass.ds(e, 1), :, :].rearrange("p e a c -> p (e a c)")
                                    ).then_inc(bias_ready, 1)
                    for r in range(RUNS):
                        base = e * U + r * KC
                        if r == 0:
                            dve.wait_ge(bias_ready, e + 1)
                        for c in range(KC):
                            dve.wait_ge(u_high, base + c + 1)
                            dve.scalar_tensor_tensor(out=ul[:, c, :], in0=ps[:, c % 2, 0:NT],
                                                     scalar=bias_now[:, UP, c:c + 1], in1=uh[:, c, :].bitcast(F32),
                                                     op0=ALU.add, op1=ALU.subtract).then_inc(u_low, 1)
                        if r == 0:
                            low(e, DOWN)
                        if r == RUNS - 1 and not last:
                            low(e + 1, UP)
                        for c in range(KC):
                            dve.wait_ge(g_silu, base + c + 1)
                            dve.wait_ge(u_sum, base + c + 1)
                            if c >= 2:
                                dve.wait_ge(g_low, base + c - 1)
                            dve.tensor_tensor(gm[:, c % 2, :], sg[:, c % 2, :], u[:, c, :], ALU.mult).then_inc(g_mul, 1)
                        if r == RUNS - 1 and not last:
                            low(e + 1, GATE)
                        for t in range(GB):
                            dve.wait_ge(o_psum, base + t + 1)
                            x = core.x[:, r * GB + t, :]
                            dve.scalar_tensor_tensor(
                                out=x, in0=ps[0:S, 4 + t, :],
                                scalar=pg[:, r * GB + t, bass.ds(e, 1)],
                                in1=x, op0=ALU.mult, op1=ALU.add).then_inc(o_add, 1)

                low(0, UP)
                low(0, GATE)
                with dve.Fori(0, EA - 1) as e:
                    expert(e)
                expert(EA - 1, True)


def store(core, out):
    stored = core.sem("stored")
    with core.nc.Block() as block:
        @block.sync
        def _(sp):
            sp.dma_start(out.rearrange("b s d -> s b d"), core.x[:]).then_inc(stored, 16)
            sp.wait_ge(stored, 16)


def build(nc, x, ctx_512, g_xattn, g_ffn, w_pack, rope_q, rope_k, w_ffn, w_att,
          w_exp, b_exp, b_down, w_router, b_router, order, out):
    with ExitStack() as ctx:
        core = Core(nc, ctx)
        for half in range(2):
            latent_attention(core, half, x, ctx_512, g_xattn, g_ffn, w_pack, rope_q, rope_k, half == 0)
            core.end_stage()
        quantised_ffn(core, w_ffn)
        core.end_stage()
        causal_attention(core, ctx_512, w_att)
        core.end_stage()
        expert_ffn(core, w_exp, b_exp, b_down, w_router, b_router, order)
        store(core, out)


def rope_tables(np, length, dim):
    inv = np.float32(1.0) / np.float32(10000.0) ** (np.arange(0, dim, 2, dtype=np.float32) / np.float32(dim))
    f = np.arange(length, dtype=np.float32)[:, None] * inv[None, :].astype(np.float32)
    return (np.repeat(np.sin(f), 2, axis=-1).astype(np.float32),
            np.repeat(np.cos(f), 2, axis=-1).astype(np.float32))


def layouts(np, inputs):
    a = {k: np.asarray(v) for k, v in inputs.items()}
    arrays = {k: np.ascontiguousarray(a[k]) for k in ("x", "ctx_512", "g_xattn", "g_ffn")}
    wq = a["L0_xattn_Wq"].reshape(PAIRS, 256, KC, 128).transpose(0, 3, 2, 1).reshape(PAIRS, 128, -1)
    kc = a["L0_xattn_w_kc_q"].reshape(PAIRS, 2, DK, CQ).transpose(0, 2, 1, 3).reshape(PAIRS, 128, -1)
    wr = a["L0_xattn_W_qr"]
    wr = np.stack([wr, np.roll(wr, -(CQ // 2), axis=1)], 0)
    wr = wr.reshape(2, PAIRS, 2, CB, 128, R).transpose(1, 4, 0, 3, 2, 5).reshape(PAIRS, 128, -1)
    kr = a["L0_xattn_W_kr"].reshape(PAIRS, 2, DC, R).transpose(0, 1, 3, 2).reshape(PAIRS, 2 * R, DC)
    kv = a["L0_xattn_w_kc_kv"].reshape(PAIRS, 2, DK, DC).transpose(0, 2, 1, 3).reshape(PAIRS, 128, -1)
    wo = a["L0_xattn_Wo"].T.reshape(PAIRS, 2, DK, D).transpose(0, 2, 1, 3).reshape(PAIRS, 128, -1)
    arrays["w_pack"] = np.ascontiguousarray(np.concatenate([wq, kc, wr, kr, kv, wo], axis=2))
    sin, cos = rope_tables(np, S, CQ)
    sin = np.roll(sin, -(CQ // 2), axis=1)
    sin[:, CQ // 2:] *= -1
    arrays["rope_q"] = np.ascontiguousarray(
        np.stack([cos, sin], 0).reshape(2, S, CB, 128).transpose(3, 0, 2, 1))
    sin, cos = rope_tables(np, L, DC)
    sin[:, :DC // 2] *= -1
    t = np.zeros((2, LCN * LC, DC), np.float32)
    t[:, :L] = np.stack([cos, sin], 0)
    arrays["rope_k"] = np.ascontiguousarray(t.reshape(2, LCN, LC, DC).transpose(2, 0, 1, 3))
    gate, up, down = (a["L0_ffn_w_" + k].T for k in ("gate", "up", "down"))
    arrays["w_ffn"] = np.ascontiguousarray(np.stack(
        [w.reshape(-1, 128, w.shape[1]).transpose(1, 0, 2).reshape(128, -1) for w in (gate, up, down)], 0))
    blocks = lambda w: w.reshape(-1, 128, w.shape[1]).transpose(1, 0, 2).reshape(128, -1)
    kv = a["L1_xattn_Wkv_expand"].T
    arrays["w_att"] = np.ascontiguousarray(np.concatenate(
        [blocks(a["L1_xattn_Wq"].T), blocks(a["L1_xattn_Wout"].T), kv], axis=1))
    names = (("Wup", "Wsu"), ("Wgate", "Wsg"), ("Wdown", "Wsd"))
    arrays["w_exp"] = np.ascontiguousarray(np.stack(
        [[blocks(w) for w in (a["L1_ffn_" + n][e] if e < E else a["L1_ffn_" + m] for n, m in names)]
         for e in range(EA)], 0))
    bias = np.stack([np.concatenate([a["L1_ffn_" + n], a["L1_ffn_" + m][None]], 0)
                     for n, m in (("bup", "bsu"), ("bgate", "bsg"))], 1)
    arrays["b_exp"] = np.ascontiguousarray(bias.reshape(EA, 2, KC, 128).transpose(3, 0, 1, 2))
    arrays["b_down"] = np.ascontiguousarray(np.concatenate([a["L1_ffn_bdown"], a["L1_ffn_bsd"][None]], 0))
    wr = np.zeros((D, EA), np.float32)
    wr[:, :E] = a["L1_ffn_Wr"]
    arrays["w_router"] = np.ascontiguousarray(wr.reshape(KC, 128, EA).transpose(1, 0, 2))
    arrays["b_router"] = np.ascontiguousarray(np.stack([a["L1_ffn_br"], a["L1_ffn_gate_bias"]], 0))
    arrays["order"] = np.arange(E, 0, -1).astype(np.float32)
    return arrays


def kernel(**inputs):
    import numpy as np
    import concourse.bacc as bacc
    from concourse.bass_utils import run_bass_kernel_spmd

    nc = bacc.Bacc("TRN2", target_bir_lowering=False, num_devices=1)
    arrays = layouts(np, inputs)
    aps = {name: nc.dram_tensor(name, a.shape, mybir.dt.from_np(a.dtype), kind="ExternalInput").ap()
           for name, a in arrays.items()}
    out = nc.dram_tensor("out", (B, S, D), F32, kind="ExternalOutput").ap()
    build(nc, out=out, **aps)
    return run_bass_kernel_spmd(nc, [arrays], core_ids=[0]).results[0]["out"]
```

```python
from contextlib import ExitStack

import concourse.bass as bass
from concourse import mybir
from concourse.alu_op_type import AluOpType as ALU

F32 = mybir.dt.float32
F32R = mybir.dt.float32r
BF16 = mybir.dt.bfloat16
ACT = mybir.ActivationFunctionType
AX = mybir.AxisListType

B, S, D = 16, 100, 512
L, DC = 361, 128
LE = L + L % 2
KC = D // 128
EPS = 1e-5

H0, DK, CQ, R = 16, 128, 384, 64
PAIRS = H0 // 2
CB = CQ // 128
LC, LCN = 121, 3
HB = B // 2
HT = HB * S
NT = 400
GB = NT // S

W_Q, W_KC, W_R = 0, KC * 256, KC * 256 + 2 * CQ
W_KR = W_R + 2 * CB * 2 * R
W_KV = W_KR + DC
W_O = W_KV + 2 * DC
W_ALL = W_O + 2 * D


class Core:

    def __init__(self, nc, ctx):
        self.nc, self.ctx, self.stage_sems = nc, ctx, []
        self.x = self.sbuf("residual", [S, B, D])
        self.ident = self.sbuf("identity", [128, 128])
        self.zero = self.sbuf("zero", [128, 1])
        self.eps = self.sbuf("eps", [128, 1])
        self.gates = self.sbuf("tanh_gates", [128, 4])
        self.mv = self.sbuf("mean_var", [S, B, 2])
        self.rstd = self.sbuf("rstd", [S, B])
        self.nmr = self.sbuf("minus_mean_rstd", [S, B])
        self.stats = self.sbuf("bn_stats", [S, B, 6])
        self.std = self.sbuf("std", [S, B])
        self.ps = ctx.enter_context(nc.psum_tensor("banks", [128, 8, 512], F32))

    def sbuf(self, name, shape, dt=F32, ctx=None):
        return (ctx or self.ctx).enter_context(self.nc.sbuf_tensor(name, shape, dt))

    def sem(self, name):
        s = self.nc.alloc_semaphore(name)
        self.stage_sems.append(s)
        return s

    def end_stage(self):
        self.nc.clear_and_free_semaphores(self.stage_sems)
        self.stage_sems = []
        self.nc.all_engine_barrier()


class NormSems:

    def __init__(self, core, tag):
        self.bn = core.sem(tag + "_bn")
        self.var = core.sem(tag + "_var")
        self.std = core.sem(tag + "_std")
        self.rstd = core.sem(tag + "_rstd")


def norm_stats_dve(dve, core, s, tiles):
    lo, hi = tiles.start, tiles.stop
    n = hi - lo
    for t in tiles:
        dve.bn_stats(core.stats[:, t, :], core.x[:, t, :]).then_inc(s.bn, 1)
    for k, t in enumerate(tiles):
        dve.wait_ge(s.bn, k + 1)
        dve.bn_aggr(core.mv[:, t, :], core.stats[:, t, :]).then_inc(s.var, 1)
    dve.wait_ge(s.std, 1)
    v, y = core.mv[:, lo:hi, 1], core.rstd[:, lo:hi]
    tmp, m = core.std[:, lo:hi], core.nmr[:, lo:hi]
    steps = [
        lambda: dve.reciprocal(y, tmp),
        lambda: dve.tensor_tensor(tmp, y, y, ALU.mult),
        lambda: dve.scalar_tensor_tensor(out=tmp, in0=v, scalar=EPS, in1=tmp, op0=ALU.add, op1=ALU.mult),
        lambda: dve.tensor_scalar(tmp, tmp, -0.5, 1.5, ALU.mult, ALU.add),
        lambda: dve.tensor_tensor(y, y, tmp, ALU.mult),
        lambda: dve.scalar_tensor_tensor(out=m, in0=core.mv[:, lo:hi, 0], scalar=-1.0, in1=y,
                                         op0=ALU.mult, op1=ALU.mult),
    ]
    for k, step in enumerate(steps):
        step().then_inc(s.rstd, 1)
        dve.wait_ge(s.rstd, k + 1)


def norm_stats_act(act, core, s, tiles):
    act.wait_ge(s.var, len(tiles))
    act.activation(core.std[:, tiles.start:tiles.stop], core.mv[:, tiles.start:tiles.stop, 1],
                   ACT.Sqrt, bias=core.eps[0:S, 0:1]).then_inc(s.std, 1)


def latent_attention(core, half, x_in, ctx_in, g_x, g_f, w_pack, rope_q, rope_k, first):
    nc, ps = core.nc, core.ps
    tag = f"la{half}_"
    b0 = half * HB
    tiles = range(b0, b0 + HB)
    with ExitStack() as own:
        def sb(name, shape, dt=F32):
            return core.sbuf(tag + name, shape, dt, own)

        def sem(name):
            return core.sem(tag + name)

        xth = sb("xn_t_high", [128, KC, HT], F32R)
        xtl = sb("xn_t_low", [128, KC, HT], F32R)
        kvh = sb("kv_t_high", [DC, HB, LE], F32R)
        kvl = sb("kv_t_low", [DC, HB, LE], F32R)
        kv = sb("kv_rows", [LC, HB, LCN, DC])
        wts = [sb(f"weights{i}", [128, W_ALL]) for i in range(2)]
        wqh, wql = sb("wq_high", [128, KC, 256], F32R), sb("wq_low", [128, KC, 256], F32R)
        wch, wcl = sb("wkc_high", [128, 2 * CQ], F32R), sb("wkc_low", [128, 2 * CQ], F32R)
        mh, ml = sb("wout_high", [DC, 2, D], F32R), sb("wout_low", [DC, 2, D], F32R)
        qh, ql = sb("q_high", [DK, 2, NT], F32R), sb("q_low", [DK, 2, NT], F32R)
        roped = sb("q_roped", [128, 2, 2, CB, NT])
        rank = sb("q_rank", [2 * R, NT])
        kh, kl = sb("qk_high", [DC, 2, HT], F32R), sb("qk_low", [DC, 2, HT], F32R)
        ch, cl = sb("ctx_high", [DC, 2, 2, S], F32R), sb("ctx_low", [DC, 2, 2, S], F32R)
        prob = sb("probs", [S, 4, LC * LCN])
        probt = sb("probs_t", [LC, 2, LCN, 2, S])
        nmax, sums, rsum = sb("minus_max", [S, 4]), sb("sums", [S, 4]), sb("rsum", [S, 4])
        trig = sb("rope_q", [128, 2, CB, S])
        warm = sb("table_warmer", [1, 1])
        flat = roped[:, :, :, :, :].rearrange("p a b c n -> p (a b c n)")
        raw = flat[0:LC, 0:HB * LCN * DC].rearrange("p (b c d) -> p b c d", b=HB, c=LCN)
        trigk = wts[1][0:LC, 0:2 * LCN * DC].rearrange("p (t c d) -> p t c d", t=2, c=LCN)
        turned = wts[1][0:LC, 2 * LCN * DC:4 * LCN * DC].rearrange("p (i c d) -> p i c d", i=2, c=LCN)
        xn = [wts[1][0:S, 4 * LCN * DC + i * D:4 * LCN * DC + (i + 1) * D] for i in range(2)]

        ns = NormSems(core, tag)
        x_loaded, const_ready = sem("x_loaded"), sem("const_ready")
        pads_zero, kv_loaded, tabs = sem("pads_zero"), sem("kv_loaded"), sem("tables_loaded")
        ident_zero = sem("ident_zero")
        turn, kept, kv_roped = sem("turn"), sem("kept"), sem("kv_roped")
        kv_t, kv_high, kv_low = sem("kv_transposed"), sem("kv_high"), sem("kv_low")
        normed, x_t, x_high, x_low = sem("normed"), sem("x_transposed"), sem("x_high"), sem("x_low")
        w_in = [sem(f"weights_in{i}") for i in range(2)]
        w_high, w_split = sem("weights_high"), sem("weights_split")
        w0 = wts[0]
        parts0 = ((w0[:, W_Q:W_KC], wqh[:].rearrange("p k c -> p (k c)"), wql[:].rearrange("p k c -> p (k c)")),
                  (w0[:, W_KC:W_R], wch[:], wcl[:]))
        with nc.Block() as block:
            @block.sync
            def _(sp):
                if first:
                    sp.dma_start(core.x[:], x_in.rearrange("b s d -> s b d")).then_inc(x_loaded, 16)
                sp.wait_ge(pads_zero, 1)
                for c in range(LCN):
                    n = min(LC, L - c * LC)
                    sp.dma_start(raw[0:n, :, c, :],
                                 ctx_in[b0:b0 + HB, c * LC:c * LC + n, :].rearrange("b p d -> p b d")
                                 ).then_inc(kv_loaded, 16)
                sp.dma_start(w0[:], w_pack[0]).then_inc(w_in[0], 16)

            @block.scalar
            def _(act):
                act.dma_start(trigk, rope_k).then_inc(tabs, 16)
                act.dma_start(trig[:], rope_q).then_inc(tabs, 16)
                if first:
                    act.dma_start(core.gates[:, 0:2], g_x.rearrange("(a n) -> a n", a=1)
                                  .to_broadcast([128, 2])).then_inc(tabs, 16)
                    act.dma_start(core.gates[:, 2:4], g_f.rearrange("(a n) -> a n", a=1)
                                  .to_broadcast([128, 2])).then_inc(tabs, 16)
                    act.wait_ge(tabs, 64)
                    act.activation(core.gates[:], core.gates[:], ACT.Tanh).then_inc(const_ready, 1)
                    act.wait_ge(const_ready, 2)
                norm_stats_act(act, core, ns, tiles)
                for i in range(HB):
                    act.wait_ge(x_t, i + 1)
                    act.copy(xth[:, :, i * S:(i + 1) * S],
                             ps[:, i % 2, 0:KC * S].rearrange("p (k s) -> p k s", k=KC)).then_inc(x_high, 1)
                    act.wait_ge(kv_t, i + 1)
                    act.copy(kvh[:, i, 0:L], ps[:, 2 + i % 2, 0:L]).then_inc(kv_high, 1)
                    if i == HB - 3:
                        act.wait_ge(w_in[0], 16)
                        for w, high, _low in parts0:
                            act.copy(high, w).then_inc(w_high, 1)

            @block.gpsimd
            def _(pool):
                pool.memset(raw[:, :, LCN - 1, :], 0.0).then_inc(pads_zero, 1)
                pool.memset(prob[:, :, L:LC * LCN], 0.0)
                pool.memset(kvh[:, :, L:LE].bitcast(F32), 0.0)
                pool.memset(kvl[:, :, L:LE].bitcast(F32), 0.0)
                if first:
                    pool.memset(core.zero[:], 0.0)
                    pool.memset(core.eps[:], EPS).then_inc(const_ready, 1)
                    pool.memset(core.ident[:], 0.0).then_inc(ident_zero, 1)
                    pool.wait_ge(ident_zero, 1)
                    pool.affine_select(out=core.ident[:], in_=core.ident[:], compare_op=ALU.not_equal,
                                       fill=1.0, base=0, pattern=[[-1, 128]],
                                       channel_multiplier=1).then_inc(ident_zero, 1)
                pool.wait_ge(tabs, 32 if not first else 64)
                pool.wait_ge(kv_loaded, 16 * LCN)
                half_d = DC // 2
                for i in range(HB):
                    t = turned[:, i % 2]
                    pool.tensor_tensor(t[:, :, 0:half_d], raw[:, i, :, half_d:DC],
                                       trigk[:, 1, :, 0:half_d], ALU.mult).then_inc(turn, 1)
                    pool.tensor_tensor(t[:, :, half_d:DC], raw[:, i, :, 0:half_d],
                                       trigk[:, 1, :, half_d:DC], ALU.mult).then_inc(turn, 1)
                    pool.wait_ge(turn, 2 * (i + 1))
                    pool.wait_ge(kept, i + 1)
                    pool.tensor_tensor(kv[:, i], kv[:, i], t, ALU.add).then_inc(kv_roped, 1)

            def low_parts(dve, i):
                dve.wait_ge(x_high, i + 1)
                dve.tensor_tensor(xtl[:, :, i * S:(i + 1) * S],
                                  ps[:, i % 2, 0:KC * S].rearrange("p (k s) -> p k s", k=KC),
                                  xth[:, :, i * S:(i + 1) * S].bitcast(F32), ALU.subtract).then_inc(x_low, 1)
                dve.wait_ge(kv_high, i + 1)
                dve.tensor_tensor(kvl[:, i, 0:L], ps[:, 2 + i % 2, 0:L], kvh[:, i, 0:L].bitcast(F32),
                                  ALU.subtract).then_inc(kv_low, 1)

            @block.vector
            def _(dve):
                if first:
                    dve.wait_ge(x_loaded, 16)
                norm_stats_dve(dve, core, ns, tiles)
                dve.wait_ge(tabs, 32 if not first else 64)
                dve.wait_ge(kv_loaded, 16 * LCN)
                for i, t in enumerate(tiles):
                    dve.tensor_tensor(kv[:, i], raw[:, i], trigk[:, 0], ALU.mult).then_inc(kept, 1)
                    if i >= 2:
                        dve.wait_ge(x_t, i - 1)
                    dve.tensor_scalar(xn[i % 2], core.x[:, t, :], core.rstd[:, t:t + 1],
                                      core.nmr[:, t:t + 1], ALU.mult, ALU.add).then_inc(normed, 1)
                    if i >= 1:
                        low_parts(dve, i - 1)
                for k, (w, high, low) in enumerate(parts0):
                    dve.wait_ge(w_high, k + 1)
                    dve.tensor_tensor(low, w, high.bitcast(F32), ALU.subtract).then_inc(w_split, 1)
                low_parts(dve, HB - 1)

            @block.tensor
            def _(pe):
                if first:
                    pe.wait_ge(ident_zero, 2)
                for i in range(HB):
                    pe.wait_ge(normed, i + 1)
                    if i >= 2:
                        pe.wait_ge(x_low, i - 1)
                    for k in range(KC):
                        mm = pe.transpose(ps[:, i % 2, k * S:(k + 1) * S], xn[i % 2][:, k * 128:(k + 1) * 128],
                                          core.ident[0:S, 0:S])
                    mm.then_inc(x_t, 1)
                    pe.wait_ge(kv_roped, i + 1)
                    if i >= 2:
                        pe.wait_ge(kv_low, i - 1)
                    for c in range(LCN):
                        n = min(LC, L - c * LC)
                        mm = pe.transpose(ps[:, 2 + i % 2, c * LC:c * LC + n], kv[0:n, i, c, :],
                                          core.ident[0:n, 0:n])
                    mm.then_inc(kv_t, 1)

        m_psum, m_high, m_low = sem("wout_psum"), sem("wout_high"), sem("wout_low")
        a_psum, a_high, a_low = sem("q_psum"), sem("q_high"), sem("q_low")
        b_psum, b_done = sem("qbig_psum"), sem("qbig_roped")
        c_psum, c_done, c_block = sem("rank_psum"), sem("rank_out"), sem("rank_blocks")
        k_psum, k_high, k_low = sem("qk_psum"), sem("qk_high"), sem("qk_low")
        s_psum, s_max, s_exp = sem("scores"), sem("scores_max"), sem("scores_exp")
        s_rec, s_norm = sem("rsum"), sem("probs_normed")
        t_psum, t_out = sem("probs_t_psum"), sem("probs_t_out")
        v_psum, v_high, v_low = sem("ctx_psum"), sem("ctx_high"), sem("ctx_low")
        o_psum, o_add = sem("out_psum"), sem("out_added")
        UNITS = 2 * (HT // NT)
        ITEMS = 2 * HB
        MIX, OUT = 5, 8
        SLOTS = OUT + ITEMS - 1
        AHEAD = (SLOTS - 6, SLOTS - 2)
        WIDEN_LAST = (0, 1)
        NARROW = (3, 4)
        ABSORB = 5
        T_BANK, V_BANK, O_BANK = 2, 4, 6
        C_BANKS = (5, O_BANK)
        B_BANKS = (3, 7)
        K_BANKS = ((T_BANK, O_BANK), B_BANKS)

        def wview(par):
            w = wts[par]
            return dict(
                q=w[:, W_Q:W_KC], kc=w[:, W_KC:W_R],
                r=w[:, W_R:W_KR].rearrange("p (v c h r) -> p v c h r", v=2, c=CB, h=2),
                kr=w[:, W_KR:W_KV],
                kv=w[:, W_KV:W_O].rearrange("p (h d) -> p h d", h=2),
                o=w[:, W_O:W_ALL].rearrange("p (h d) -> p h d", h=2))

        with nc.Block() as block:
            @block.sync
            def _(sp):
                sp.dma_start(wts[1][:], w_pack[1]).then_inc(w_in[1], 16)
                with sp.Fori(1, PAIRS // 2) as i:
                    for par in range(2):
                        n = i * 2 + par
                        sp.wait_ge(k_psum, (n - 1) * UNITS)
                        sp.dma_start(wts[par][:], w_pack[n]).then_inc(w_in[par], 16)

            @block.gpsimd
            def _(pool):
                def split(n, i, par):
                    w = wview(par)
                    pool.wait_ge(w_in[par], (i + 1) * 16)
                    pool.wait_ge(a_psum, n * UNITS)
                    pool.tensor_tensor(wqh[:].rearrange("p k c -> p (k c)"), w["q"],
                                       core.zero[:, 0:1].to_broadcast([128, KC * 256]), ALU.add).then_inc(w_high, 1)
                    pool.wait_ge(w_high, n * 2 + 1)
                    pool.tensor_tensor(wql[:].rearrange("p k c -> p (k c)"), w["q"],
                                       wqh[:].rearrange("p k c -> p (k c)").bitcast(F32),
                                       ALU.subtract).then_inc(w_split, 1)
                    pool.wait_ge(b_psum, n * UNITS * CB)
                    pool.tensor_tensor(wch[:], w["kc"], core.zero[:, 0:1].to_broadcast([128, 2 * CQ]),
                                       ALU.add).then_inc(w_high, 1)
                    pool.wait_ge(w_high, n * 2 + 2)
                    pool.tensor_tensor(wcl[:], w["kc"], wch[:].bitcast(F32),
                                       ALU.subtract).then_inc(w_split, 1)

                split(1, 0, 1)
                with pool.Fori(1, PAIRS // 2) as i:
                    for par in range(2):
                        split(i * 2 + par, i, par)

            @block.tensor
            def _(pe):
                def project(n, u, blocks=range(KC)):
                    run, h = u // 2, u % 2
                    if u >= 2 and 0 in blocks:
                        pe.wait_ge(a_low, n * UNITS + u - 1)
                    for k in blocks:
                        xs = slice(run * NT, (run + 1) * NT)
                        wc = slice(h * 128, (h + 1) * 128)
                        for j, (a, b) in enumerate(((wqh, xth), (wqh, xtl), (wql, xth))):
                            mm = pe.matmul(ps[:, u % 2, 0:NT], a[:, k, wc], b[:, k, xs],
                                           start=(k == 0 and j == 0), stop=(k == KC - 1 and j == 2))
                    if KC - 1 in blocks:
                        mm.then_inc(a_psum, 1)

                def widen(n, u, c):
                    h, k = u % 2, u * CB + c
                    if c == 0:
                        pe.wait_ge(a_low, n * UNITS + u + 1)
                    if k >= 2:
                        pe.wait_ge(b_done, (n * UNITS * CB + k - 1) * 2)
                    wc = slice(h * CQ + c * 128, h * CQ + (c + 1) * 128)
                    for j, (a, b) in enumerate(((wch, qh), (wch, ql), (wcl, qh))):
                        mm = pe.matmul(ps[:, B_BANKS[k % 2], 0:NT], a[:, wc], b[:, u % 2, :],
                                       start=(j == 0), stop=(j == 2))
                    mm.then_inc(b_psum, 1)

                def narrow(n, run, w, part, parts):
                    steps = [(v, c) for c in range(CB) for v in range(2)]
                    each = len(steps) // parts
                    if part == 0:
                        pe.wait_ge(b_done, (n * UNITS + 2 * run + 2) * CB * 2)
                    for j in range(part * each, (part + 1) * each):
                        v, c = steps[j]
                        for h in range(2):
                            mm = pe.matmul(ps[h * R:(h + 1) * R, C_BANKS[run], 0:NT], w["r"][:, v, c, h, :],
                                           roped[:, h, v, c, :], start=(j == 0), stop=(j == 2 * CB - 1),
                                           skip_group_check=True)
                        if j == 2 * CB - 1:
                            mm.then_inc(c_psum, 1)
                        elif run == 0 and v == 1:
                            mm.then_inc(c_block, 1)

                def absorb(n, run, w):
                    pe.wait_ge(c_done, n * (UNITS // 2) + run + 1)
                    for h in range(2):
                        pe.matmul(ps[:, K_BANKS[run][h], 0:NT], w["kr"][h * R:(h + 1) * R, :],
                                  rank[h * R:(h + 1) * R, :], start=True, stop=True).then_inc(k_psum, 1)

                def wout(w, h):
                    pe.matmul(ps[:, 4 + h, :], w["kv"][:, h, :], w["o"][:, h, :],
                              start=True, stop=True).then_inc(m_psum, 1)

                def scores(n, j):
                    b, h = j // 2, j % 2
                    pe.wait_ge(k_low, n * UNITS + 2 * (b // GB) + h + 1)
                    if j >= 2:
                        pe.wait_ge(s_exp, n * ITEMS + j - 1)
                    qs = slice(b * S, (b + 1) * S)
                    for k, (a, c) in enumerate(((kh, kvh), (kh, kvl), (kl, kvh))):
                        mm = pe.matmul(ps[0:S, j % 2, 0:LE], a[:, h, qs], c[:, b, :],
                                       start=(k == 0), stop=(k == 2))
                    mm.then_inc(s_psum, 1)

                def turn_probs(n, j):
                    pe.wait_ge(s_norm, n * ITEMS + j + 1)
                    if j >= 1:
                        pe.wait_ge(t_out, n * ITEMS + j)
                    for c in range(LCN):
                        mm = pe.transpose(ps[0:LC, T_BANK, c * S:(c + 1) * S],
                                          prob[:, j % 4, c * LC:(c + 1) * LC], core.ident[0:S, 0:S])
                    mm.then_inc(t_psum, 1)

                def mix(n, b):
                    pe.wait_ge(t_out, n * ITEMS + 2 * b + 2)
                    if b >= 1:
                        pe.wait_ge(v_low, n * HB + b)
                    else:
                        pe.wait_ge(m_low, n * 2 + 1)
                    for c in range(LCN):
                        mm = pe.matmul(ps[:, V_BANK, 0:2 * S], kv[:, b, c, :],
                                       probt[:, b % 2, c, :, :].rearrange("p h s -> p (h s)"),
                                       start=(c == 0), stop=(c == LCN - 1))
                    mm.then_inc(v_psum, 1)

                def out(n, b):
                    pe.wait_ge(v_low, n * HB + b + 1)
                    if b == 0:
                        pe.wait_ge(m_low, n * 2 + 2)
                    else:
                        pe.wait_ge(o_add, n * HB + b)
                    for h in range(2):
                        for j, (a, c) in enumerate(((ch, mh), (ch, ml), (cl, mh))):
                            mm = pe.matmul(ps[0:S, O_BANK, :], a[:, b % 2, h, :], c[:, h, :],
                                           start=(h == 0 and j == 0), stop=(h == 1 and j == 2))
                    mm.then_inc(o_psum, 1)

                def first_units(n, u):
                    pe.wait_ge(w_split, n * 2 + 1)
                    pe.wait_ge(s_exp, n * ITEMS + u - 1)
                    project(n, u)

                def pair(n, i, par, last=False):
                    w = wview(par)
                    pe.wait_ge(w_in[par], (i + 1) * 16)
                    pe.wait_ge(w_split, n * 2 + 2)
                    lo, hi = range(KC // 2), range(KC // 2, KC)
                    widen(n, 0, 0)
                    widen(n, 0, 1)
                    project(n, 2, lo)
                    widen(n, 0, 2)
                    project(n, 2, hi)
                    widen(n, 1, 0)
                    widen(n, 1, 1)
                    project(n, 3, lo)
                    widen(n, 1, 2)
                    project(n, 3, hi)
                    widen(n, 2, 0)
                    widen(n, 2, 1)
                    narrow(n, 0, w, 0, 1)
                    widen(n, 2, 2)
                    wout(w, 0)
                    absorb(n, 0, w)
                    widen(n, 3, 0)
                    wout(w, 1)
                    for s in range(SLOTS):
                        if s < ITEMS:
                            scores(n, s)
                        if s in WIDEN_LAST:
                            widen(n, 3, 1 + WIDEN_LAST.index(s))
                        if s in range(MIX, MIX + ITEMS, 2):
                            mix(n, (s - MIX) // 2)
                        if s == ABSORB:
                            absorb(n, 1, w)
                        if s in range(OUT, OUT + ITEMS, 2):
                            out(n, (s - OUT) // 2)
                        if s in NARROW:
                            narrow(n, 1, w, NARROW.index(s), len(NARROW))
                        if 2 <= s < ITEMS + 2:
                            turn_probs(n, s - 2)
                        if s in AHEAD and not last:
                            first_units(n + 1, AHEAD.index(s))

                project(0, 0)
                project(0, 1)
                with pe.Fori(0, PAIRS // 2 - 1) as i:
                    for par in range(2):
                        pair(i * 2 + par, i, par)
                pair(PAIRS - 2, PAIRS // 2 - 1, 0)
                pair(PAIRS - 1, PAIRS // 2 - 1, 1, last=True)

            @block.scalar
            def _(act):
                def high(n, u):
                    act.wait_ge(a_psum, n * UNITS + u + 1)
                    if u >= 2:
                        act.wait_ge(b_psum, (n * UNITS + u - 1) * CB)
                    act.copy(qh[:, u % 2, :], ps[:, u % 2, 0:NT]).then_inc(a_high, 1)

                def rank_out(n, run):
                    act.wait_ge(c_psum, n * (UNITS // 2) + run + 1)
                    act.copy(rank[:], ps[:, C_BANKS[run], 0:NT]).then_inc(c_done, 1)

                def qk_high(n, run):
                    for h in range(2):
                        act.wait_ge(k_psum, n * UNITS + 2 * run + h + 1)
                        act.copy(kh[:, h, run * NT:(run + 1) * NT],
                                 ps[:, K_BANKS[run][h], 0:NT]).then_inc(k_high, 1)

                def wout_high(n, h):
                    act.wait_ge(m_psum, n * 2 + h + 1)
                    act.activation(mh[:, h, :], ps[:, 4 + h, :], ACT.Copy,
                                   scale=core.gates[:, 0:1]).then_inc(m_high, 1)

                def pair(n, last=False, early=True):
                    if early:
                        act.copy(warm[:], core.zero[0:1, 0:1])
                    high(n, 2)
                    high(n, 3)
                    rank_out(n, 0)
                    qk_high(n, 0)
                    wout_high(n, 0)
                    for s in range(SLOTS):
                        if s < ITEMS:
                            act.wait_ge(s_max, n * ITEMS + s + 1)
                            if s >= 4:
                                act.wait_ge(t_psum, n * ITEMS + s - 3)
                            act.activation(prob[:, s % 4, 0:L], ps[0:S, s % 2, 0:L], ACT.Exp,
                                           bias=nmax[:, s % 4:s % 4 + 1],
                                           accum_out=sums[:, s % 4:s % 4 + 1]).then_inc(s_exp, 1)
                        if s == 0:
                            wout_high(n, 1)
                        if s in range(MIX, MIX + ITEMS, 2):
                            b = (s - MIX) // 2
                            act.wait_ge(v_psum, n * HB + b + 1)
                            if b >= 2:
                                act.wait_ge(o_psum, n * HB + b - 1)
                            act.copy(ch[:, b % 2, :, :].rearrange("p h s -> p (h s)"),
                                     ps[:, V_BANK, 0:2 * S]).then_inc(v_high, 1)
                        if 2 <= s < ITEMS + 2:
                            j = s - 2
                            b = j // 2
                            act.wait_ge(t_psum, n * ITEMS + j + 1)
                            if b >= 2:
                                act.wait_ge(v_psum, n * HB + b - 1)
                            act.copy(probt[:, b % 2, :, j % 2, :],
                                     ps[0:LC, T_BANK, 0:LCN * S].rearrange("p (c s) -> p c s", c=LCN)
                                     ).then_inc(t_out, 1)
                        if s == NARROW[-1]:
                            rank_out(n, 1)
                        if s == ABSORB:
                            qk_high(n, 1)
                        if s in AHEAD and not last:
                            high(n + 1, AHEAD.index(s))

                high(0, 0)
                high(0, 1)
                with act.Fori(0, PAIRS // 2 - 1) as i:
                    for par in range(2):
                        pair(i * 2 + par, early=par == 0)
                pair(PAIRS - 2)
                pair(PAIRS - 1, last=True, early=False)

            @block.vector
            def _(dve):
                def low(n, u):
                    dve.wait_ge(a_high, n * UNITS + u + 1)
                    dve.tensor_tensor(ql[:, u % 2, :], ps[:, u % 2, 0:NT], qh[:, u % 2, :].bitcast(F32),
                                      ALU.subtract).then_inc(a_low, 1)

                def rope(n, u, c):
                    run, h = u // 2, u % 2
                    k = u * CB + c
                    if u == 2 and c < CB - 1:
                        dve.wait_ge(c_block, n * (CB - 1) + c + 1)
                    elif u == 2:
                        dve.wait_ge(c_psum, n * (UNITS // 2) + 1)
                    dve.wait_ge(b_psum, n * UNITS * CB + k + 1)
                    for v in range(2):
                        dve.tensor_tensor(
                            roped[:, h, v, c, :].rearrange("p (b s) -> p b s", b=GB),
                            ps[:, B_BANKS[k % 2], 0:NT].rearrange("p (b s) -> p b s", b=GB),
                            trig[:, v, c, :].unsqueeze(1).to_broadcast([128, GB, S]),
                            ALU.mult).then_inc(b_done, 1)

                def qk_low(n, run, h):
                    dve.wait_ge(k_high, n * UNITS + 2 * run + h + 1)
                    rs = slice(run * NT, (run + 1) * NT)
                    dve.tensor_tensor(kl[:, h, rs], ps[:, K_BANKS[run][h], 0:NT],
                                      kh[:, h, rs].bitcast(F32), ALU.subtract).then_inc(k_low, 1)

                def wout_low(n, h):
                    dve.wait_ge(m_high, n * 2 + h + 1)
                    dve.scalar_tensor_tensor(out=ml[:, h, :], in0=ps[:, 4 + h, :],
                                             scalar=core.gates[:, 0:1], in1=mh[:, h, :].bitcast(F32),
                                             op0=ALU.mult, op1=ALU.subtract).then_inc(m_low, 1)

                def pair(n, last=False):
                    rope(n, 0, 0)
                    rope(n, 0, 1)
                    rope(n, 0, 2)
                    low(n, 2)
                    rope(n, 1, 0)
                    rope(n, 1, 1)
                    rope(n, 1, 2)
                    low(n, 3)
                    for c in range(CB):
                        rope(n, 2, c)
                    qk_low(n, 0, 0)
                    qk_low(n, 0, 1)
                    rope(n, 3, 0)
                    for s in range(SLOTS):
                        if s < ITEMS:
                            dve.wait_ge(s_psum, n * ITEMS + s + 1)
                            dve.tensor_reduce(nmax[:, s % 4:s % 4 + 1], ps[0:S, s % 2, 0:L], AX.X, ALU.max,
                                              negate=True).then_inc(s_max, 1)
                        if 1 <= s < ITEMS + 1:
                            j = s - 1
                            dve.wait_ge(s_exp, n * ITEMS + j + 1)
                            dve.reciprocal(rsum[:, j % 4:j % 4 + 1], sums[:, j % 4:j % 4 + 1]).then_inc(s_rec, 1)
                            dve.wait_ge(s_rec, n * ITEMS + j + 1)
                            dve.tensor_scalar(prob[:, j % 4, 0:L], prob[:, j % 4, 0:L],
                                              rsum[:, j % 4:j % 4 + 1], None, ALU.mult).then_inc(s_norm, 1)
                        if s in WIDEN_LAST:
                            rope(n, 3, 1 + WIDEN_LAST.index(s))
                        if s in (MIX - 2, MIX - 1):
                            wout_low(n, s - MIX + 2)
                        if s in (ABSORB + 1, ABSORB + 2):
                            qk_low(n, 1, s - ABSORB - 1)
                        if s in range(MIX, MIX + ITEMS, 2):
                            b = (s - MIX) // 2
                            dve.wait_ge(v_high, n * HB + b + 1)
                            dve.tensor_tensor(cl[:, b % 2, :, :].rearrange("p h s -> p (h s)"),
                                              ps[:, V_BANK, 0:2 * S],
                                              ch[:, b % 2, :, :].rearrange("p h s -> p (h s)").bitcast(F32),
                                              ALU.subtract).then_inc(v_low, 1)
                        if s in range(OUT, OUT + ITEMS, 2):
                            b = (s - OUT) // 2
                            dve.wait_ge(o_psum, n * HB + b + 1)
                            x = core.x[:, b0 + b, :]
                            dve.tensor_tensor(x, x, ps[0:S, O_BANK, :], ALU.add).then_inc(o_add, 1)
                        if s in AHEAD and not last:
                            low(n + 1, AHEAD.index(s))

                low(0, 0)
                low(0, 1)
                with dve.Fori(0, PAIRS // 2 - 1) as i:
                    for par in range(2):
                        pair(i * 2 + par)
                pair(PAIRS - 2)
                pair(PAIRS - 1, last=True)


DI = 2048
IC = DI // 128
NC = DI // 512
ROUND = 12582912.0
W_COUNT = float(DI * D)


def quantised_ffn(core, w_ffn):
    nc, ps = core.nc, core.ps
    tag = "qf_"
    GATE, UP, DOWN = range(3)
    with ExitStack() as own:
        def sb(name, shape, dt=F32):
            return core.sbuf(tag + name, shape, dt, own)

        def sem(name):
            return core.sem(tag + name)

        raw = sb("raw_weights", [128, 2, KC * DI])
        wq = sb("sign_weights", [128, 3, KC * DI], BF16)
        xqt = sb("x_quant_t", [128, KC, B * S], BF16)
        wsum, wscale, winv = sb("w_abs_sums", [128, 3]), sb("w_scale", [128, 3]), sb("w_inverse", [128, 3])
        ones = sb("ones", [128, 128])
        identb = sb("identity_bf16", [128, 128], BF16)
        rnd = sb("rounder", [128, 1])
        xmax, xscale, xinv = sb("x_max", [S, B]), sb("x_scale", [S, B]), sb("x_inverse", [S, B])
        gscale, uscale = sb("gate_scale", [S, B]), sb("up_scale", [S, B])
        hmax, hscale, hinv = sb("h_max", [S, 2]), sb("h_scale", [S, 2]), sb("h_inverse", [S, 2])
        oscale = sb("out_scale", [S, 2])
        dscale = sb("down_scale", [128, 1])
        h = sb("hidden", [S, 2, DI])
        hq = sb("hidden_quant", [S, 2, DI], BF16)
        hqt = sb("hidden_quant_t", [128, 2, IC, S], BF16)
        XG = DI // D
        xn = [h[:, i, :].rearrange("p (t d) -> p t d", t=XG) for i in range(2)]
        xq = [hq[:, i, :].rearrange("p (t d) -> p t d", t=XG) for i in range(2)]
        HALF = KC * DI // 2
        ns = NormSems(core, tag)
        loaded = [sem(f"w_loaded{i}") for i in range(3)]
        consts = sem("consts")
        w_abs, w_tot, w_inv, w_small = sem("w_abs"), sem("w_total"), sem("w_inv"), sem("w_small")
        w_up, w_clip, w_done = sem("w_scaled"), sem("w_clipped"), sem("w_done")
        n_done, n_max, n_small, n_mul, n_q = sem("normed"), sem("x_absmax"), sem("x_small"), sem("x_scaled"), sem("x_quant")
        x_t, x_done = sem("x_transposed"), sem("x_t_out")
        scales = sem("scales")

        def psb(t):
            return ps[:, t % 2, :].bitcast(BF16)[:, 0:KC * S].rearrange("p (k s) -> p k s", k=KC)

        with nc.Block() as block:
            @block.sync
            def _(sp):
                for m in range(2):
                    sp.dma_start(raw[:, m, :], w_ffn[m]).then_inc(loaded[m], 16)
                for p in range(2):
                    sp.wait_ge(w_done, p + 1)
                    hs = slice(p * HALF, (p + 1) * HALF)
                    sp.dma_start(raw[:, 0, hs], w_ffn[2][:, hs]).then_inc(loaded[2], 16)

            @block.gpsimd
            def _(pool):
                pool.memset(ones[:], 1.0).then_inc(consts, 1)
                pool.memset(rnd[:], ROUND).then_inc(consts, 1)
                pool.tensor_copy(identb[:], core.ident[:]).then_inc(consts, 1)
                pool.wait_ge(ns.rstd, 6)
                for g in range(B // XG):
                    if g >= 2:
                        pool.wait_ge(n_q, g - 1)
                    for k in range(XG):
                        t = g * XG + k
                        pool.tensor_scalar(xn[g % 2][:, k, :], core.x[:, t, :], core.rstd[:, t:t + 1],
                                           core.nmr[:, t:t + 1], ALU.mult, ALU.add).then_inc(n_done, 1)

            @block.scalar
            def _(act):
                norm_stats_act(act, core, ns, range(B))
                act.wait_ge(consts, 3)

                def weight_sum(m):
                    act.wait_ge(loaded[m], 16 * (1 + m // 2))
                    act.activation(wq[:, m, :], raw[:, m % 2, :], ACT.Abs,
                                   accum_out=wsum[:, m:m + 1]).then_inc(w_abs, 1)

                def weight_round(m):
                    act.wait_ge(w_inv, m + 1)
                    for p in range(2):
                        hs = slice(p * HALF, (p + 1) * HALF)
                        act.activation(raw[:, m % 2, hs], raw[:, m % 2, hs], ACT.Identity, bias=rnd[:, 0:1],
                                       scale=winv[:, m:m + 1]).then_inc(w_up, 1)

                def x_round(g):
                    act.wait_ge(n_small, 2 * g + 2)
                    for k in range(XG):
                        t = g * XG + k
                        act.activation(xn[g % 2][:, k, :], xn[g % 2][:, k, :], ACT.Identity,
                                       bias=rnd[0:S, 0:1], scale=xinv[:, t:t + 1]).then_inc(n_mul, 1)

                weight_sum(0)
                weight_round(0)
                x_round(0)
                x_round(1)
                weight_sum(1)
                weight_round(1)
                x_round(2)
                x_round(3)
                weight_sum(2)
                weight_round(2)

            @block.vector
            def _(dve):
                norm_stats_dve(dve, core, ns, range(B))
                small = [0]

                def chain(ins):
                    small[0] += 1
                    ins.then_inc(w_small, 1)
                    dve.wait_ge(w_small, small[0])

                def inverse(m):
                    dve.wait_ge(w_tot, m + 1)
                    chain(dve.tensor_scalar(wscale[:, m:m + 1], ps[:, 5 + m, 0:1], 1.0 / W_COUNT, EPS,
                                            ALU.mult, ALU.add))
                    dve.reciprocal(winv[:, m:m + 1], wscale[:, m:m + 1]).then_inc(w_inv, 1)

                def quantise(m):
                    for p in range(2):
                        hs, k = slice(p * HALF, (p + 1) * HALF), 2 * m + p + 1
                        dve.wait_ge(w_up, k)
                        dve.tensor_scalar(raw[:, m % 2, hs], raw[:, m % 2, hs], ROUND - 1.0, ROUND + 1.0,
                                          ALU.max, ALU.min).then_inc(w_clip, 1)
                        dve.wait_ge(w_clip, k)
                        dve.tensor_scalar(wq[:, m, hs], raw[:, m % 2, hs], ROUND, None,
                                          ALU.subtract).then_inc(w_done, 1)

                def x_scales(g):
                    gt = slice(g * XG, (g + 1) * XG)
                    dve.wait_ge(n_done, (g + 1) * XG)
                    dve.tensor_reduce(xmax[:, gt], xn[g % 2], AX.X, ALU.max,
                                      apply_absolute_value=True).then_inc(n_max, 1)
                    dve.wait_ge(n_max, g + 1)
                    dve.tensor_scalar(xscale[:, gt], xmax[:, gt], 1.0 / 127.0, EPS,
                                      ALU.mult, ALU.add).then_inc(n_small, 1)
                    dve.wait_ge(n_small, 2 * g + 1)
                    dve.reciprocal(xinv[:, gt], xscale[:, gt]).then_inc(n_small, 1)

                def x_quantise(g):
                    dve.wait_ge(n_mul, (g + 1) * XG)
                    if g >= 2:
                        dve.wait_ge(x_t, (g - 1) * XG)
                    dve.tensor_scalar(xq[g % 2], xn[g % 2], ROUND, 127.0,
                                      ALU.subtract, ALU.min).then_inc(n_q, 1)

                def x_turned(g):
                    for t in range(g * XG, (g + 1) * XG):
                        dve.wait_ge(x_t, t + 1)
                        dve.tensor_copy(xqt[:, :, t * S:(t + 1) * S], psb(t)).then_inc(x_done, 1)

                x_scales(0)
                x_scales(1)
                inverse(0)
                quantise(0)
                x_quantise(0)
                x_quantise(1)
                x_turned(0)
                x_turned(1)
                inverse(1)
                x_scales(2)
                x_scales(3)
                quantise(1)
                x_quantise(2)
                x_quantise(3)
                x_turned(2)
                x_turned(3)
                inverse(2)
                quantise(2)
                dve.tensor_scalar(gscale[:], xscale[:], wscale[0:S, GATE:GATE + 1], None, ALU.mult).then_inc(scales, 1)
                dve.tensor_scalar(uscale[:], xscale[:], wscale[0:S, UP:UP + 1], None, ALU.mult).then_inc(scales, 1)
                dve.tensor_scalar(dscale[:], wscale[:, DOWN:DOWN + 1], core.gates[:, 2:3], None,
                                  ALU.mult).then_inc(scales, 1)

            @block.tensor
            def _(pe):
                pe.wait_ge(consts, 3)

                def total(m):
                    pe.wait_ge(w_abs, m + 1)
                    pe.matmul(ps[:, 5 + m, 0:1], ones[:], wsum[:, m:m + 1], start=True, stop=True).then_inc(w_tot, 1)

                def turn_x(g):
                    pe.wait_ge(n_q, g + 1)
                    for t in range(g * XG, (g + 1) * XG):
                        if t >= 2:
                            pe.wait_ge(x_done, t - 1)
                        for k in range(KC):
                            mm = pe.transpose(psb(t)[:, k, :], xq[g % 2][:, t % XG, k * 128:(k + 1) * 128],
                                              identb[0:S, 0:S])
                        mm.then_inc(x_t, 1)

                total(0)
                turn_x(0)
                turn_x(1)
                total(1)
                turn_x(2)
                turn_x(3)
                total(2)

        gs, gs_ready = sb("gate_scale_of_tile", [S, 2]), sem("gate_scale_ready")
        g_psum, u_psum, g_out, u_out = sem("gate_psum"), sem("up_psum"), sem("gate_out"), sem("up_out")
        h_max, h_small, h_mul, h_q = sem("h_absmax"), sem("h_small"), sem("h_scaled"), sem("h_quant")
        t_psum, t_out = sem("h_t_psum"), sem("h_t_out")
        o_psum, o_add = sem("out_psum"), sem("out_added")

        def pst(half):
            return ps[:, 4 + half, :].bitcast(BF16)[:, 0:IC // 2 * S].rearrange("p (k s) -> p k s", k=IC // 2)

        with nc.Block() as block:
            @block.tensor
            def _(pe):
                def widen(t, blocks=range(NC), first=False):
                    for c in blocks:
                        for m, bank, psum, read in ((GATE, 0, g_psum, g_out), (UP, 2, u_psum, u_out)):
                            if c >= 2 or not first:
                                pe.wait_ge(read, t * NC + c - 1)
                            for k in range(KC):
                                mm = pe.matmul(ps[0:S, bank + c % 2, :], xqt[:, k, bass.ds(t * S, S)],
                                               wq[:, m, k * DI + c * 512:k * DI + (c + 1) * 512],
                                               start=(k == 0), stop=(k == KC - 1))
                            mm.then_inc(psum, 1)

                def turn(t, par, first=False):
                    pe.wait_ge(h_q, t + 1)
                    for half in range(2):
                        if not first:
                            pe.wait_ge(t_out, t * 2 + half - 1)
                        for k in range(IC // 2):
                            i = half * (IC // 2) + k
                            mm = pe.transpose(pst(half)[:, k, :], hq[:, par, i * 128:(i + 1) * 128],
                                              identb[0:S, 0:S])
                        mm.then_inc(t_psum, 1)

                def narrow(t, par):
                    pe.wait_ge(t_out, t * 2 + 2)
                    for i in range(IC):
                        mm = pe.matmul(ps[0:S, 6 + par, :], hqt[:, par, i, :], wq[:, DOWN, i * D:(i + 1) * D],
                                       start=(i == 0), stop=(i == IC - 1))
                    mm.then_inc(o_psum, 1)

                def tile(t, par, first=False):
                    widen(t, range(NC - 1))
                    turn(t - 1, 1 - par, first)
                    widen(t, range(NC - 1, NC))
                    narrow(t - 1, 1 - par)

                widen(0, first=True)
                tile(1, 1, True)
                with pe.Fori(0, B // 2 - 1) as i:
                    for par in range(2):
                        tile(i * 2 + par + 2, par)
                turn(B - 1, 1)
                narrow(B - 1, 1)

            @block.scalar
            def _(act):
                def own_scale(t, par):
                    act.copy(gs[:, par:par + 1], gscale[:, bass.ds(t, 1)]).then_inc(gs_ready, 1)

                def widen(t, par, c):
                    act.wait_ge(gs_ready, t + 1)
                    act.wait_ge(g_psum, t * NC + c + 1)
                    act.activation(h[:, par, c * 512:(c + 1) * 512], ps[0:S, c % 2, :], ACT.Silu,
                                   scale=gs[:, par:par + 1]).then_inc(g_out, 1)

                def turn(t, par):
                    for half in range(2):
                        act.wait_ge(t_psum, t * 2 + half + 1)
                        act.copy(hqt[:, par, half * (IC // 2):(half + 1) * (IC // 2), :], pst(half)).then_inc(t_out, 1)

                def tile(t, par):
                    own_scale(t, par)
                    for c in range(NC - 1):
                        widen(t, par, c)
                    turn(t - 1, 1 - par)
                    widen(t, par, NC - 1)

                own_scale(0, 0)
                for c in range(NC):
                    widen(0, 0, c)
                tile(1, 1)
                with act.Fori(0, B // 2 - 1) as i:
                    for par in range(2):
                        tile(i * 2 + par + 2, par)
                turn(B - 1, 1)

            @block.vector
            def _(dve):
                def widen(t, par):
                    for c in range(NC):
                        cs = slice(c * 512, (c + 1) * 512)
                        dve.wait_ge(u_psum, t * NC + c + 1)
                        dve.wait_ge(g_out, t * NC + c + 1)
                        dve.scalar_tensor_tensor(out=h[:, par, cs], in0=ps[0:S, 2 + c % 2, :],
                                                 scalar=uscale[:, bass.ds(t, 1)], in1=h[:, par, cs],
                                                 op0=ALU.mult, op1=ALU.mult).then_inc(u_out, 1)

                def quantise(t, par):
                    k = slice(par, par + 1)
                    dve.wait_ge(u_out, t * NC + NC)
                    dve.tensor_reduce(hmax[:, k], h[:, par, :], AX.X, ALU.max,
                                      apply_absolute_value=True).then_inc(h_max, 1)
                    dve.wait_ge(h_max, t + 1)
                    dve.tensor_scalar(hscale[:, k], hmax[:, k], 1.0 / 127.0, EPS,
                                      ALU.mult, ALU.add).then_inc(h_small, 1)
                    dve.wait_ge(h_small, t * 3 + 1)
                    dve.reciprocal(hinv[:, k], hscale[:, k]).then_inc(h_small, 1)
                    dve.tensor_scalar(oscale[:, k], hscale[:, k], dscale[0:S, 0:1], None,
                                      ALU.mult).then_inc(h_small, 1)
                    dve.wait_ge(h_small, t * 3 + 3)
                    dve.tensor_scalar(h[:, par, :], h[:, par, :], hinv[:, k], ROUND,
                                      ALU.mult, ALU.add).then_inc(h_mul, 1)
                    dve.wait_ge(h_mul, t + 1)
                    dve.tensor_scalar(hq[:, par, :], h[:, par, :], ROUND, 127.0,
                                      ALU.subtract, ALU.min).then_inc(h_q, 1)

                def add(t, par):
                    dve.wait_ge(o_psum, t + 1)
                    x = core.x[:, bass.ds(t, 1), :].rearrange("p t d -> p (t d)")
                    dve.scalar_tensor_tensor(out=x, in0=ps[0:S, 6 + par, :], scalar=oscale[:, par:par + 1],
                                             in1=x, op0=ALU.mult, op1=ALU.add).then_inc(o_add, 1)

                widen(0, 0)
                quantise(0, 0)
                widen(1, 1)
                quantise(1, 1)
                with dve.Fori(0, B // 2 - 1) as i:
                    for par in range(2):
                        t = i * 2 + par
                        widen(t + 2, par)
                        add(t, par)
                        quantise(t + 2, par)
                add(B - 2, 0)
                add(B - 1, 1)


H1 = 16
HD = D // H1
HPB = 128 // HD
A_Q, A_O, A_K, A_V = 0, KC * D, 2 * KC * D, 2 * KC * D + D
A_ALL = A_V + D
FAR = -3.0e38


def causal_attention(core, ctx_in, w_att):
    nc, ps = core.nc, core.ps
    tag = "ca_"
    with ExitStack() as own:
        def sb(name, shape, dt=F32):
            return core.sbuf(tag + name, shape, dt, own)

        def sem(name):
            return core.sem(tag + name)

        w = sb("weights", [128, A_ALL])
        wqh, wql = sb("wq_high", [128, KC, D], F32R), sb("wq_low", [128, KC, D], F32R)
        woh, wol = sb("wo_high", [128, KC, D], F32R), sb("wo_low", [128, KC, D], F32R)
        lat = sb("latents", [S, B, DC])
        xn = sb("xn", [S, 2, D])
        xth, xtl = sb("xn_t_high", [128, KC, NT], F32R), sb("xn_t_low", [128, KC, NT], F32R)
        latt = sb("latents_t", [DC, GB, S])
        lats = sb("latents_now", [S, GB, DC])
        qt = sb("q_t", [128, KC, GB, S])
        kt = sb("k_t_by_head", [128, GB, KC, HPB, S])
        v = sb("values", [S, 2, D])
        p = sb("probs", [S, 4, HPB, S])
        pt = sb("probs_t", [S, 2, KC, HPB, S])
        oh, ol = sb("heads_high", [128, 2, KC, S], F32R), sb("heads_low", [128, 2, KC, S], F32R)
        mask = sb("mask", [S, S])
        mx, sm, rs = sb("minus_maxima", [S, 4, HPB]), sb("sums", [S, 4, HPB]), sb("rsums", [S, 4, HPB])
        ns = NormSems(core, tag)
        w_in, l_in, mask_zero, consts = sem("weights_in"), sem("latents_in"), sem("mask_zero"), sem("consts")
        w_high, w_low = sem("weights_high"), sem("weights_low")
        normed, x_t, x_high, x_low = sem("normed"), sem("x_transposed"), sem("x_high"), sem("x_low")
        l_now, l_t, l_out = sem("latents_moved"), sem("latents_transposed"), sem("latents_t_out")
        q_psum, q_out, k_psum, k_out = sem("q_psum"), sem("q_out"), sem("k_psum"), sem("k_out")
        v_psum, v_out = sem("v_psum"), sem("v_out")
        s_psum, s_mask, s_max = sem("scores"), sem("scores_masked"), sem("scores_max")
        s_exp, s_sum, s_rec, s_norm = sem("scores_exp"), sem("exp_sum"), sem("rsum"), sem("probs_normed")
        t_psum, t_out = sem("probs_t_psum"), sem("probs_t_out")
        m_psum, m_high, m_low = sem("heads_psum"), sem("heads_high"), sem("heads_low")
        o_psum, o_add = sem("out_psum"), sem("out_added")
        ITEMS = GB * KC
        SLOTS = ITEMS + 6
        PV_AT, OUT_AT = 7, 9

        with nc.Block() as block:
            @block.sync
            def _(sp):
                sp.dma_start(w[:], w_att).then_inc(w_in, 16)
                sp.dma_start(lat[:], ctx_in[:, 0:S, :].rearrange("b p d -> p b d")).then_inc(l_in, 16)

            @block.gpsimd
            def _(pool):
                pool.memset(kt[:], 0.0).then_inc(consts, 1)
                pool.memset(mask[:], 0.0).then_inc(mask_zero, 1)
                pool.wait_ge(mask_zero, 1)
                pool.affine_select(out=mask[:], in_=mask[:], compare_op=ALU.is_ge, fill=FAR, base=0,
                                   pattern=[[-1, S]], channel_multiplier=1).then_inc(consts, 1)

            @block.scalar
            def _(act):
                act.wait_ge(w_in, 16)
                for high, at in ((wqh, A_Q), (woh, A_O)):
                    act.copy(high[:].rearrange("p k d -> p (k d)"), w[:, at:at + KC * D]).then_inc(w_high, 1)
                norm_stats_act(act, core, ns, range(B))

            @block.vector
            def _(dve):
                norm_stats_dve(dve, core, ns, range(B))
                for k, (high, low, at) in enumerate(((wqh, wql, A_Q), (woh, wol, A_O))):
                    hv, lv = (a[:].rearrange("p k d -> p (k d)") for a in (high, low))
                    dve.wait_ge(w_high, k + 1)
                    dve.tensor_tensor(lv, w[:, at:at + KC * D], hv.bitcast(F32), ALU.subtract).then_inc(w_low, 1)
                dve.wait_ge(l_in, 16)

        with nc.Block() as block:
            @block.tensor
            def _(pe):
                def scores(g, j):
                    b, c = j // KC, j % KC
                    if j >= 2:
                        pe.wait_ge(s_mask, g * ITEMS + j - 1)
                    pe.matmul(ps[0:S, j % 2, 0:NT], qt[:, c, b, :],
                              kt[:, b, c, :, :].rearrange("p h s -> p (h s)"),
                              start=True, stop=True).then_inc(s_psum, 1)

                def values(g, b):
                    if b >= 1:
                        pe.wait_ge(v_out, g * GB + b)
                    pe.matmul(ps[0:S, 4, :], latt[:, b, :], w[:, A_V:A_ALL],
                              start=True, stop=True).then_inc(v_psum, 1)

                def turn(g, j):
                    pe.wait_ge(s_norm, g * ITEMS + j + 1)
                    if j >= 2:
                        pe.wait_ge(t_out, g * ITEMS + j - 1)
                    for h in range(HPB):
                        mm = pe.transpose(ps[0:S, 2 + j % 2, h * S:(h + 1) * S], p[:, j % 4, h, :],
                                          core.ident[0:S, 0:S])
                    mm.then_inc(t_psum, 1)

                def mix(g, b):
                    pe.wait_ge(t_out, g * ITEMS + (b + 1) * KC)
                    pe.wait_ge(v_out, g * GB + b + 1)
                    for c in range(KC):
                        for h in range(HPB):
                            at = c * 128 + h * HD
                            mm = pe.matmul(ps[h * HD:(h + 1) * HD, 5, c * S:(c + 1) * S],
                                           v[:, b % 2, at:at + HD], pt[:, b % 2, c, h, :],
                                           start=True, stop=True)
                    mm.then_inc(m_psum, 1)

                def out(g, b):
                    pe.wait_ge(m_low, g * GB + b + 1)
                    if b >= 2:
                        pe.wait_ge(o_add, g * GB + b - 1)
                    for c in range(KC):
                        for k, (a, m) in enumerate(((oh, woh), (oh, wol), (ol, woh))):
                            mm = pe.matmul(ps[0:S, 6 + b % 2, :], a[:, b % 2, c, :], m[:, c, :],
                                           start=(c == 0 and k == 0), stop=(c == KC - 1 and k == 2))
                    mm.then_inc(o_psum, 1)

                def turn_x(g, t):
                    pe.wait_ge(normed, g * GB + t + 1)
                    if t >= 2:
                        pe.wait_ge(x_low, g * GB + t - 1)
                    for k in range(KC):
                        mm = pe.transpose(ps[:, 2 + t % 2, k * S:(k + 1) * S], xn[:, t % 2, k * 128:(k + 1) * 128],
                                          core.ident[0:S, 0:S])
                    mm.then_inc(x_t, 1)

                def queries(g, c):
                    if c >= 2:
                        pe.wait_ge(q_out, g * KC + c - 1)
                    for k in range(KC):
                        for i, (a, x) in enumerate(((wqh, xth), (wqh, xtl), (wql, xth))):
                            mm = pe.matmul(ps[:, 4 + c % 2, 0:NT], a[:, k, c * 128:(c + 1) * 128], x[:, k, :],
                                           start=(k == 0 and i == 0), stop=(k == KC - 1 and i == 2))
                    mm.then_inc(q_psum, 1)

                def keys(g, c):
                    if c >= 2:
                        pe.wait_ge(k_out, g * KC * HPB + (c - 1) * HPB)
                    pe.matmul(ps[:, c % 2, 0:NT], w[:, A_K + c * 128:A_K + (c + 1) * 128],
                              latt[:].rearrange("p b s -> p (b s)"), start=True, stop=True).then_inc(k_psum, 1)

                with pe.Fori(0, B // GB) as g:
                    turn_x(g, 0)
                    pe.wait_ge(l_now, g + 1)
                    for t in range(GB):
                        mm = pe.transpose(ps[:, 4, t * S:(t + 1) * S], lats[:, t, :], core.ident[0:S, 0:S])
                    mm.then_inc(l_t, 1)
                    turn_x(g, 1)
                    pe.wait_ge(l_out, g + 1)
                    keys(g, 0)
                    turn_x(g, 2)
                    keys(g, 1)
                    turn_x(g, 3)
                    pe.wait_ge(x_low, g * GB + GB)
                    queries(g, 0)
                    keys(g, 2)
                    queries(g, 1)
                    keys(g, 3)
                    queries(g, 2)
                    queries(g, 3)
                    pe.wait_ge(q_out, g * KC + KC)
                    pe.wait_ge(k_out, (g + 1) * KC * HPB)
                    for s in range(SLOTS):
                        if s < ITEMS:
                            scores(g, s)
                            if s % KC == 0:
                                values(g, s // KC)
                        if 3 <= s < ITEMS + 3:
                            turn(g, s - 3)
                        if s >= PV_AT and (s - PV_AT) % KC == 0:
                            mix(g, (s - PV_AT) // KC)
                        if s >= OUT_AT and (s - OUT_AT) % KC == 0:
                            out(g, (s - OUT_AT) // KC)

            @block.scalar
            def _(act):
                def x_part(g, t):
                    act.wait_ge(x_t, g * GB + t + 1)
                    act.copy(xth[:, :, t * S:(t + 1) * S],
                             ps[:, 2 + t % 2, 0:KC * S].rearrange("p (k s) -> p k s", k=KC)).then_inc(x_high, 1)

                def keys(g, c):
                    act.wait_ge(k_psum, g * KC + c + 1)
                    for h in range(HPB):
                        hp = slice(h * HD, (h + 1) * HD)
                        act.copy(kt[hp, :, c, h, :],
                                 ps[hp, c % 2, 0:NT].rearrange("p (b s) -> p b s", b=GB)).then_inc(k_out, 1)

                def queries(g, c):
                    act.wait_ge(q_psum, g * KC + c + 1)
                    act.activation(qt[:, c].rearrange("p b s -> p (b s)"), ps[:, 4 + c % 2, 0:NT], ACT.Copy,
                                   scale=float(HD) ** -0.5).then_inc(q_out, 1)

                with act.Fori(0, B // GB) as g:
                    x_part(g, 0)
                    act.wait_ge(l_t, g + 1)
                    act.copy(latt[:].rearrange("p b s -> p (b s)"), ps[:, 4, 0:GB * S]).then_inc(l_out, 1)
                    x_part(g, 1)
                    keys(g, 0)
                    x_part(g, 2)
                    keys(g, 1)
                    x_part(g, 3)
                    queries(g, 0)
                    keys(g, 2)
                    queries(g, 1)
                    keys(g, 3)
                    queries(g, 2)
                    queries(g, 3)
                    for s in range(SLOTS):
                        if 3 <= s < ITEMS + 3:
                            j = s - 3
                            b = j // KC
                            act.wait_ge(t_psum, g * ITEMS + j + 1)
                            if b >= 2:
                                act.wait_ge(m_psum, g * GB + b - 1)
                            act.copy(pt[:, b % 2, j % KC].rearrange("p h s -> p (h s)"),
                                     ps[0:S, 2 + j % 2, 0:NT]).then_inc(t_out, 1)
                        if s < ITEMS:
                            act.wait_ge(s_max, g * ITEMS + s + 1)
                            for h in range(HPB):
                                act.activation(p[:, s % 4, h, :], p[:, s % 4, h, :], ACT.Exp,
                                               bias=mx[:, s % 4, h:h + 1]).then_inc(s_exp, 1)
                        if s >= PV_AT and (s - PV_AT) % KC == 0:
                            b = (s - PV_AT) // KC
                            act.wait_ge(m_psum, g * GB + b + 1)
                            if b >= 2:
                                act.wait_ge(o_psum, g * GB + b - 1)
                            act.activation(oh[:, b % 2].rearrange("p c s -> p (c s)"), ps[:, 5, 0:KC * S],
                                           ACT.Copy, scale=core.gates[:, 1:2]).then_inc(m_high, 1)

            @block.gpsimd
            def _(pool):
                with pool.Fori(0, B // GB) as g:
                    for j in range(ITEMS):
                        k = j % 4
                        pool.wait_ge(s_rec, g * ITEMS + j + 1)
                        pool.tensor_tensor(p[:, k], p[:, k], rs[:, k].unsqueeze(2).to_broadcast([S, HPB, S]),
                                           ALU.mult).then_inc(s_norm, 1)

            @block.vector
            def _(dve):
                with dve.Fori(0, B // GB) as g:
                    for t in range(GB):
                        if t >= 2:
                            dve.wait_ge(x_t, g * GB + t - 1)
                        at = g * GB + t
                        dve.tensor_scalar(xn[:, t % 2, :], core.x[:, bass.ds(at, 1), :].rearrange("p t d -> p (t d)"),
                                          core.rstd[:, bass.ds(at, 1)], core.nmr[:, bass.ds(at, 1)],
                                          ALU.mult, ALU.add).then_inc(normed, 1)
                        if t == 0:
                            dve.tensor_copy(lats[:], lat[:, bass.ds(g * GB, GB), :]).then_inc(l_now, 1)
                        if t >= 1:
                            dve.wait_ge(x_high, g * GB + t)
                            dve.tensor_tensor(xtl[:, :, (t - 1) * S:t * S],
                                              ps[:, 2 + (t - 1) % 2, 0:KC * S].rearrange("p (k s) -> p k s", k=KC),
                                              xth[:, :, (t - 1) * S:t * S].bitcast(F32), ALU.subtract).then_inc(x_low, 1)
                    dve.wait_ge(x_high, g * GB + GB)
                    dve.tensor_tensor(xtl[:, :, (GB - 1) * S:],
                                      ps[:, 2 + (GB - 1) % 2, 0:KC * S].rearrange("p (k s) -> p k s", k=KC),
                                      xth[:, :, (GB - 1) * S:].bitcast(F32), ALU.subtract).then_inc(x_low, 1)
                    for s in range(SLOTS):
                        if 2 <= s < ITEMS + 2:
                            j = s - 2
                            k = j % 4
                            dve.wait_ge(s_exp, (g * ITEMS + j + 1) * HPB)
                            dve.tensor_reduce(sm[:, k], p[:, k], AX.X, ALU.add).then_inc(s_sum, 1)
                            dve.wait_ge(s_sum, g * ITEMS + j + 1)
                            dve.reciprocal(rs[:, k], sm[:, k]).then_inc(s_rec, 1)
                        if s < ITEMS:
                            k = s % 4
                            dve.wait_ge(s_psum, g * ITEMS + s + 1)
                            dve.tensor_tensor(p[:, k], ps[0:S, s % 2, 0:NT].rearrange("p (h s) -> p h s", h=HPB),
                                              mask[:].unsqueeze(1).to_broadcast([S, HPB, S]),
                                              ALU.add).then_inc(s_mask, 1)
                            dve.wait_ge(s_mask, g * ITEMS + s + 1)
                            dve.tensor_reduce(mx[:, k], p[:, k], AX.X, ALU.max,
                                              negate=True).then_inc(s_max, 1)
                            if s % KC == 0:
                                b = s // KC
                                dve.wait_ge(v_psum, g * GB + b + 1)
                                dve.tensor_copy(v[:, b % 2, :], ps[0:S, 4, :]).then_inc(v_out, 1)
                        if s >= PV_AT and (s - PV_AT) % KC == 0:
                            b = (s - PV_AT) // KC
                            dve.wait_ge(m_high, g * GB + b + 1)
                            dve.scalar_tensor_tensor(out=ol[:, b % 2].rearrange("p c s -> p (c s)"),
                                                     in0=ps[:, 5, 0:KC * S], scalar=core.gates[:, 1:2],
                                                     in1=oh[:, b % 2].rearrange("p c s -> p (c s)").bitcast(F32),
                                                     op0=ALU.mult, op1=ALU.subtract).then_inc(m_low, 1)
                        if s >= OUT_AT and (s - OUT_AT) % KC == 0:
                            b = (s - OUT_AT) // KC
                            dve.wait_ge(o_psum, g * GB + b + 1)
                            x = core.x[:, bass.ds(g * GB + b, 1), :].rearrange("p t d -> p (t d)")
                            dve.tensor_tensor(x, x, ps[0:S, 6 + b % 2, :], ALU.add).then_inc(o_add, 1)


E = 7
EA = E + 1
MATS = 3
UP, GATE, DOWN = range(MATS)


def expert_ffn(core, w_exp, b_exp, b_down, w_router, b_router, order):
    nc, ps = core.nc, core.ps
    tag = "ex_"
    with ExitStack() as own:
        def sb(name, shape, dt=F32):
            return core.sbuf(tag + name, shape, dt, own)

        def sem(name):
            return core.sem(tag + name)

        xth, xtl = sb("xn_t_high", [128, KC, B * S], F32R), sb("xn_t_low", [128, KC, B * S], F32R)
        raw = sb("raw_weights", [128, MATS, KC * D])
        wh, wl = sb("weights_high", [128, MATS, KC * D], F32R), sb("weights_low", [128, MATS, KC * D], F32R)
        bias, bias_now = sb("biases", [128, EA, 2, KC]), sb("biases_now", [128, 2, KC])
        pg = sb("gated_probs", [S, B, EA])
        uh, ul = sb("u_high", [128, KC, NT], F32R), sb("u_low", [128, KC, NT], F32R)
        u = sb("u", [128, KC, NT])
        sg, gm = sb("silu_gate", [128, 2, NT]), sb("g", [128, 2, NT])
        gh, gl = sb("g_high", [128, KC, NT], F32R), sb("g_low", [128, KC, NT], F32R)
        flat = u[:].rearrange("p k n -> p (k n)")
        xn = [flat[0:S, i * D:(i + 1) * D] for i in range(2)]
        sgf, gmf = sg[:].rearrange("p k n -> p (k n)"), gm[:].rearrange("p k n -> p (k n)")
        bd = gmf[0:EA, 0:D]
        pgt = flat[0:EA, 0:B * S].rearrange("p (t s) -> p t s", t=B)
        lgt = flat[0:EA, 2 * D:2 * D + NT]
        wr = sgf[:, 0:KC * EA].rearrange("p (k e) -> p k e", k=KC)
        wrh, wrl = sb("router_high", [128, KC, EA], F32R), sb("router_low", [128, KC, EA], F32R)
        br = sb("router_bias", [S, 2, E])
        seq = sb("order", [S, E])
        logit, biased = sb("logits", [S, B, E]), sb("biased", [S, B, E])
        one, two, hit = sb("first", [S, B, E]), sb("second", [S, B, E]), sb("hit", [S, B, E])
        top = sb("top", [S, B])
        ns = NormSems(core, tag)
        w_in = [sem(f"weights_in{m}") for m in range(MATS)]
        small_in = sem("small_in")
        r_split = sem("router_split")
        normed, x_t, x_high, x_low = sem("normed"), sem("x_transposed"), sem("x_high"), sem("x_low")
        r_psum, step_done, d_exp, r_exp = sem("router_psum"), sem("router_step"), sem("less_max"), sem("router_exp")
        pg_done, pg_t, pg_out, b_psum, b_add = sem("probs"), sem("probs_turned"), sem("probs_t_out"), sem("bias_psum"), sem("bias_added")
        l_psum, l_out = sem("logits_psum"), sem("logits_out")
        w_high, w_low = sem("weights_high"), sem("weights_low")
        bias_ready = sem("bias_ready")
        u_psum, u_high, u_low, u_sum = sem("u_psum"), sem("u_high"), sem("u_low"), sem("u_sum")
        g_psum, g_silu, g_mul, g_high, g_low = sem("g_psum"), sem("g_silu"), sem("g_mul"), sem("g_high"), sem("g_low")
        o_psum, o_add = sem("out_psum"), sem("out_added")

        def load(sp, e, m):
            sp.dma_start(raw[:, m, :], w_exp[e, m]).then_inc(w_in[m], 16)

        def high(act, e, m):
            act.wait_ge(w_in[m], (e + 1) * 16)
            act.copy(wh[:, m, :], raw[:, m, :]).then_inc(w_high, 1)

        def low(dve, e, m):
            dve.wait_ge(w_high, e * MATS + m + 1)
            dve.tensor_tensor(wl[:, m, :], raw[:, m, :], wh[:, m, :].bitcast(F32),
                              ALU.subtract).then_inc(w_low, 1)

        with nc.Block() as block:
            @block.sync
            def _(sp):
                for dst, src in ((wr, w_router), (bias[:], b_exp), (bd, b_down),
                                 (br[:].rearrange("p a e -> p (a e)"), b_router.rearrange("(o a) e -> o (a e)", o=1).to_broadcast([S, 2 * E])),
                                 (seq[:], order.rearrange("(o e) -> o e", o=1).to_broadcast([S, E]))):
                    sp.dma_start(dst, src).then_inc(small_in, 16)
                for m in range(MATS):
                    load(sp, 0, m)

            @block.scalar
            def _(act):
                def logits(r):
                    act.wait_ge(l_psum, r + 1)
                    if r >= 1:
                        act.wait_ge(r_psum, r)
                    act.copy(lgt, ps[0:EA, 4 + r, 0:NT]).then_inc(l_out, 1)

                norm_stats_act(act, core, ns, range(B))
                for t in range(B):
                    act.wait_ge(x_t, t + 1)
                    act.copy(xth[:, :, t * S:(t + 1) * S],
                             ps[:, t % 2, 0:KC * S].rearrange("p (k s) -> p k s", k=KC)).then_inc(x_high, 1)
                    if t >= GB + 2 and t % GB == 2:
                        logits(t // GB - 1)
                logits(B // GB - 1)
                high(act, 0, UP)
                high(act, 0, GATE)
                act.wait_ge(d_exp, 1)
                act.activation(hit[:], hit[:], ACT.Exp).then_inc(r_exp, 1)
                for k in range(4):
                    act.wait_ge(pg_t, k + 1)
                    act.copy(pgt[:, 4 * k:4 * k + 4, :].rearrange("p t s -> p (t s)"),
                             ps[0:EA, k, 0:4 * S]).then_inc(pg_out, 1)

            @block.vector
            def _(dve):
                norm_stats_dve(dve, core, ns, range(B))
                for t in range(B):
                    if t >= 2:
                        dve.wait_ge(x_t, t - 1)
                    dve.tensor_scalar(xn[t % 2], core.x[:, t, :], core.rstd[:, t:t + 1],
                                      core.nmr[:, t:t + 1], ALU.mult, ALU.add).then_inc(normed, 1)
                    if t >= 1:
                        dve.wait_ge(x_high, t)
                        dve.tensor_tensor(xtl[:, :, (t - 1) * S:t * S],
                                          ps[:, (t - 1) % 2, 0:KC * S].rearrange("p (k s) -> p k s", k=KC),
                                          xth[:, :, (t - 1) * S:t * S].bitcast(F32), ALU.subtract).then_inc(x_low, 1)
                    if t == 1:
                        dve.wait_ge(small_in, 80)
                        dve.tensor_copy(wrh[:], wr).then_inc(r_split, 1)
                        dve.wait_ge(r_split, 1)
                        dve.tensor_tensor(wrl[:], wr, wrh[:].bitcast(F32), ALU.subtract).then_inc(r_split, 1)
                dve.wait_ge(x_high, B)
                dve.tensor_tensor(xtl[:, :, (B - 1) * S:],
                                  ps[:, (B - 1) % 2, 0:KC * S].rearrange("p (k s) -> p k s", k=KC),
                                  xth[:, :, (B - 1) * S:].bitcast(F32), ALU.subtract).then_inc(x_low, 1)
                dve.wait_ge(r_psum, B // GB)
                done = [0]

                def step(ins):
                    done[0] += 1
                    ins.then_inc(step_done, 1)
                    dve.wait_ge(step_done, done[0])

                wide = [S, B, E]
                tops = top[:].unsqueeze(2).to_broadcast(wide)
                seqs = seq[:].unsqueeze(1).to_broadcast(wide)
                step(dve.tensor_tensor(logit[:], ps[0:S, 2, 0:B * EA].rearrange("p (t e) -> p t e", t=B)[:, :, 0:E],
                                       br[:, 0, :].unsqueeze(1).to_broadcast(wide), ALU.add))
                step(dve.tensor_tensor(biased[:], logit[:], br[:, 1, :].unsqueeze(1).to_broadcast(wide), ALU.add))
                for which in (one, two):
                    step(dve.tensor_reduce(top[:], biased[:], AX.X, ALU.max))
                    step(dve.tensor_tensor(hit[:], biased[:], tops, ALU.is_equal))
                    step(dve.tensor_tensor(hit[:], hit[:], seqs, ALU.mult))
                    step(dve.tensor_reduce(top[:], hit[:], AX.X, ALU.max))
                    step(dve.tensor_tensor(which[:], hit[:], tops, ALU.is_equal))
                    step(dve.scalar_tensor_tensor(out=biased[:], in0=which[:], scalar=FAR, in1=biased[:],
                                                  op0=ALU.mult, op1=ALU.add))
                step(dve.tensor_tensor(one[:], one[:], two[:], ALU.add))
                step(dve.tensor_scalar(one[:], one[:], -FAR, FAR, ALU.mult, ALU.add))
                step(dve.tensor_tensor(logit[:], logit[:], one[:], ALU.add))
                step(dve.tensor_reduce(top[:], logit[:], AX.X, ALU.max))
                dve.tensor_tensor(hit[:], logit[:], tops, ALU.subtract).then_inc(d_exp, 1)
                dve.wait_ge(r_exp, 1)
                step(dve.tensor_reduce(top[:], hit[:], AX.X, ALU.add))
                step(dve.reciprocal(top[:], top[:]))
                step(dve.tensor_scalar(top[:], top[:], core.gates[0:S, 3:4], None, ALU.mult))
                dve.wait_ge(pg_done, 1)
                dve.tensor_tensor(pg[:, :, 0:E], hit[:], tops, ALU.mult).then_inc(pg_done, 1)
                dve.tensor_scalar(pg[:, :, E:EA], pg[:, :, E:EA], core.gates[0:S, 3:4], None,
                                  ALU.mult).then_inc(pg_done, 1)
                low(dve, 0, UP)
                for t in range(B):
                    dve.wait_ge(b_psum, t + 1)
                    dve.tensor_tensor(core.x[:, t, :], core.x[:, t, :], ps[0:S, 4 + t % 4, :],
                                      ALU.add).then_inc(b_add, 1)
                    if t == B // 2:
                        low(dve, 0, GATE)

            @block.gpsimd
            def _(pool):
                pool.memset(pg[:], 1.0).then_inc(pg_done, 1)

            @block.tensor
            def _(pe):
                def route(r):
                    pe.wait_ge(r_split, 2)
                    pe.wait_ge(x_low, (r + 1) * GB)
                    for k in range(KC):
                        for i, (a, m) in enumerate(((xth, wrh), (xth, wrl), (xtl, wrh))):
                            mm = pe.matmul(ps[0:EA, 4 + r, 0:NT], m[:, k, :], a[:, k, r * NT:(r + 1) * NT],
                                           start=(k == 0 and i == 0), stop=(k == KC - 1 and i == 2))
                    mm.then_inc(l_psum, 1)

                def turn_logits(r):
                    pe.wait_ge(l_out, r + 1)
                    for k in range(GB):
                        t = r * GB + k
                        mm = pe.transpose(ps[0:S, 2, t * EA:(t + 1) * EA], lgt[:, k * S:(k + 1) * S],
                                          core.ident[0:EA, 0:EA])
                    mm.then_inc(r_psum, 1)

                for t in range(B):
                    pe.wait_ge(normed, t + 1)
                    if t >= 2:
                        pe.wait_ge(x_low, t - 1)
                    for k in range(KC):
                        mm = pe.transpose(ps[:, t % 2, k * S:(k + 1) * S], xn[t % 2][:, k * 128:(k + 1) * 128],
                                          core.ident[0:S, 0:S])
                    mm.then_inc(x_t, 1)
                    if t >= GB + 1 and t % GB == 1:
                        route(t // GB - 1)
                    if t >= GB + 3 and t % GB == 3:
                        turn_logits(t // GB - 1)
                route(B // GB - 1)
                turn_logits(B // GB - 1)
                pe.wait_ge(pg_done, 3)
                for t in range(B):
                    mm = pe.transpose(ps[0:EA, t // 4, t % 4 * S:(t % 4 + 1) * S], pg[:, t, :],
                                      core.ident[0:S, 0:S])
                    if t % 4 == 3:
                        mm.then_inc(pg_t, 1)
                for t in range(B):
                    pe.wait_ge(pg_out, t // 4 + 1)
                    if t >= 4:
                        pe.wait_ge(b_add, t - 3)
                    pe.matmul(ps[0:S, 4 + t % 4, :], pgt[:, t, :], bd, start=True, stop=True).then_inc(b_psum, 1)

        RUNS = B // GB
        U = RUNS * KC

        def mat(w, m):
            return w[:, m, :].rearrange("p (k d) -> p k d", k=KC)

        with nc.Block() as block:
            @block.sync
            def _(sp):
                with sp.Fori(1, EA) as e:
                    for m in range(MATS):
                        sp.wait_ge(w_low, (e - 1) * MATS + m + 1)
                        load(sp, e, m)

            @block.tensor
            def _(pe):
                passes = ((0, 0), (0, 1), (1, 0))
                with pe.Fori(0, EA) as e:
                    for r in range(RUNS):
                        base = e * U + r * KC
                        if r == 0:
                            pe.wait_ge(w_low, e * MATS + UP + 1)
                        for c in range(KC):
                            if c >= 2:
                                pe.wait_ge(u_low, base + c - 1)
                            for k in range(KC):
                                for i, (a, x) in enumerate(passes):
                                    mm = pe.matmul(ps[:, c % 2, 0:NT],
                                                   mat((wh, wl)[a], UP)[:, k, c * 128:(c + 1) * 128],
                                                   (xth, xtl)[x][:, k, r * NT:(r + 1) * NT],
                                                   start=(k == 0 and i == 0), stop=(k == KC - 1 and i == 2))
                            mm.then_inc(u_psum, 1)
                        if r == 0:
                            pe.wait_ge(w_low, e * MATS + GATE + 1)
                        for c in range(KC):
                            if c >= 2:
                                pe.wait_ge(g_silu, base + c - 1)
                            for k in range(KC):
                                if c == 0:
                                    pe.wait_ge(u_low, base + k + 1)
                                for i, (a, x) in enumerate(passes):
                                    mm = pe.matmul(ps[:, 2 + c % 2, 0:NT],
                                                   mat((wh, wl)[a], GATE)[:, k, c * 128:(c + 1) * 128],
                                                   (uh, ul)[x][:, k, :],
                                                   start=(k == 0 and i == 0), stop=(k == KC - 1 and i == 2))
                            mm.then_inc(g_psum, 1)
                        if r == 0:
                            pe.wait_ge(w_low, e * MATS + DOWN + 1)
                        for k in range(KC):
                            pe.wait_ge(g_low, base + k + 1)
                            for t in range(GB):
                                for i, (a, x) in enumerate(passes):
                                    mm = pe.matmul(ps[0:S, 4 + t, :], (gh, gl)[x][:, k, t * S:(t + 1) * S],
                                                   mat((wh, wl)[a], DOWN)[:, k, :],
                                                   start=(k == 0 and i == 0), stop=(k == KC - 1 and i == 2))
                                if k == KC - 1:
                                    mm.then_inc(o_psum, 1)

            @block.scalar
            def _(act):
                def expert(e, last=False):
                    for r in range(RUNS):
                        base = e * U + r * KC
                        if r == 0:
                            act.wait_ge(bias_ready, e + 1)
                        for c in range(KC):
                            act.wait_ge(u_psum, base + c + 1)
                            act.activation(uh[:, c, :], ps[:, c % 2, 0:NT], ACT.Identity,
                                           bias=bias_now[:, UP, c:c + 1]).then_inc(u_high, 1)
                        if r == 0:
                            high(act, e, DOWN)
                        if r == RUNS - 1 and not last:
                            high(act, e + 1, UP)
                        for c in range(KC + 1):
                            if c < KC:
                                act.wait_ge(g_psum, base + c + 1)
                                if c >= 2:
                                    act.wait_ge(g_mul, base + c - 1)
                                act.activation(sg[:, c % 2, :], ps[:, 2 + c % 2, 0:NT], ACT.Silu,
                                               bias=bias_now[:, GATE, c:c + 1]).then_inc(g_silu, 1)
                            if c >= 1:
                                act.wait_ge(g_mul, base + c)
                                act.copy(gh[:, c - 1, :], gm[:, (c - 1) % 2, :]).then_inc(g_high, 1)
                        if r == RUNS - 1 and not last:
                            high(act, e + 1, GATE)

                with act.Fori(0, EA - 1) as e:
                    expert(e)
                expert(EA - 1, True)

            @block.gpsimd
            def _(pool):
                with pool.Fori(0, EA) as e:
                    for r in range(RUNS):
                        base = e * U + r * KC
                        for c in range(KC):
                            pool.wait_ge(u_low, base + c + 1)
                            pool.tensor_tensor(u[:, c, :], uh[:, c, :].bitcast(F32), ul[:, c, :].bitcast(F32),
                                               ALU.add).then_inc(u_sum, 1)
                        for c in range(KC):
                            pool.wait_ge(g_high, base + c + 1)
                            pool.tensor_tensor(gl[:, c, :], gm[:, c % 2, :], gh[:, c, :].bitcast(F32),
                                               ALU.subtract).then_inc(g_low, 1)

            @block.vector
            def _(dve):
                def expert(e, last=False):
                    dve.tensor_copy(bias_now[:].rearrange("p a c -> p (a c)"),
                                    bias[:, bass.ds(e, 1), :, :].rearrange("p e a c -> p (e a c)")
                                    ).then_inc(bias_ready, 1)
                    for r in range(RUNS):
                        base = e * U + r * KC
                        if r == 0:
                            dve.wait_ge(bias_ready, e + 1)
                        for c in range(KC):
                            dve.wait_ge(u_high, base + c + 1)
                            dve.scalar_tensor_tensor(out=ul[:, c, :], in0=ps[:, c % 2, 0:NT],
                                                     scalar=bias_now[:, UP, c:c + 1], in1=uh[:, c, :].bitcast(F32),
                                                     op0=ALU.add, op1=ALU.subtract).then_inc(u_low, 1)
                        if r == 0:
                            low(dve, e, DOWN)
                        if r == RUNS - 1 and not last:
                            low(dve, e + 1, UP)
                        for c in range(KC):
                            dve.wait_ge(g_silu, base + c + 1)
                            dve.wait_ge(u_sum, base + c + 1)
                            if c >= 2:
                                dve.wait_ge(g_low, base + c - 1)
                            dve.tensor_tensor(gm[:, c % 2, :], sg[:, c % 2, :], u[:, c, :], ALU.mult).then_inc(g_mul, 1)
                        if r == RUNS - 1 and not last:
                            low(dve, e + 1, GATE)
                        for t in range(GB):
                            dve.wait_ge(o_psum, base + t + 1)
                            x = core.x[:, r * GB + t, :]
                            dve.scalar_tensor_tensor(
                                out=x, in0=ps[0:S, 4 + t, :],
                                scalar=pg[:, r * GB + t, bass.ds(e, 1)],
                                in1=x, op0=ALU.mult, op1=ALU.add).then_inc(o_add, 1)

                with dve.Fori(0, EA - 1) as e:
                    expert(e)
                expert(EA - 1, True)


def store(core, out):
    stored = core.sem("stored")
    with core.nc.Block() as block:
        @block.sync
        def _(sp):
            sp.dma_start(out.rearrange("b s d -> s b d"), core.x[:]).then_inc(stored, 16)
            sp.wait_ge(stored, 16)


def build(nc, x, ctx_512, g_xattn, g_ffn, w_pack, rope_q, rope_k, w_ffn, w_att,
          w_exp, b_exp, b_down, w_router, b_router, order, out):
    with ExitStack() as ctx:
        core = Core(nc, ctx)
        for half in range(2):
            latent_attention(core, half, x, ctx_512, g_xattn, g_ffn, w_pack, rope_q, rope_k, half == 0)
            core.end_stage()
        quantised_ffn(core, w_ffn)
        core.end_stage()
        causal_attention(core, ctx_512, w_att)
        core.end_stage()
        expert_ffn(core, w_exp, b_exp, b_down, w_router, b_router, order)
        store(core, out)


def rope_tables(np, length, dim):
    inv = np.float32(1.0) / np.float32(10000.0) ** (np.arange(0, dim, 2, dtype=np.float32) / np.float32(dim))
    f = np.arange(length, dtype=np.float32)[:, None] * inv[None, :].astype(np.float32)
    return (np.repeat(np.sin(f), 2, axis=-1).astype(np.float32),
            np.repeat(np.cos(f), 2, axis=-1).astype(np.float32))


def layouts(np, inputs):
    a = {k: np.asarray(v) for k, v in inputs.items()}
    arrays = {k: np.ascontiguousarray(a[k]) for k in ("x", "ctx_512", "g_xattn", "g_ffn")}
    wq = a["L0_xattn_Wq"].reshape(PAIRS, 256, KC, 128).transpose(0, 3, 2, 1).reshape(PAIRS, 128, -1)
    kc = a["L0_xattn_w_kc_q"].reshape(PAIRS, 2, DK, CQ).transpose(0, 2, 1, 3).reshape(PAIRS, 128, -1)
    wr = a["L0_xattn_W_qr"]
    wr = np.stack([wr, np.roll(wr, -(CQ // 2), axis=1)], 0)
    wr = wr.reshape(2, PAIRS, 2, CB, 128, R).transpose(1, 4, 0, 3, 2, 5).reshape(PAIRS, 128, -1)
    kr = a["L0_xattn_W_kr"].reshape(PAIRS, 2, DC, R).transpose(0, 1, 3, 2).reshape(PAIRS, 2 * R, DC)
    kv = a["L0_xattn_w_kc_kv"].reshape(PAIRS, 2, DK, DC).transpose(0, 2, 1, 3).reshape(PAIRS, 128, -1)
    wo = a["L0_xattn_Wo"].T.reshape(PAIRS, 2, DK, D).transpose(0, 2, 1, 3).reshape(PAIRS, 128, -1)
    arrays["w_pack"] = np.ascontiguousarray(np.concatenate([wq, kc, wr, kr, kv, wo], axis=2))
    sin, cos = rope_tables(np, S, CQ)
    sin = np.roll(sin, -(CQ // 2), axis=1)
    sin[:, CQ // 2:] *= -1
    arrays["rope_q"] = np.ascontiguousarray(
        np.stack([cos, sin], 0).reshape(2, S, CB, 128).transpose(3, 0, 2, 1))
    sin, cos = rope_tables(np, L, DC)
    sin[:, :DC // 2] *= -1
    t = np.zeros((2, LCN * LC, DC), np.float32)
    t[:, :L] = np.stack([cos, sin], 0)
    arrays["rope_k"] = np.ascontiguousarray(t.reshape(2, LCN, LC, DC).transpose(2, 0, 1, 3))
    gate, up, down = (a["L0_ffn_w_" + k].T for k in ("gate", "up", "down"))
    arrays["w_ffn"] = np.ascontiguousarray(np.stack(
        [w.reshape(-1, 128, w.shape[1]).transpose(1, 0, 2).reshape(128, -1) for w in (gate, up, down)], 0))
    blocks = lambda w: w.reshape(-1, 128, w.shape[1]).transpose(1, 0, 2).reshape(128, -1)
    kv = a["L1_xattn_Wkv_expand"].T
    arrays["w_att"] = np.ascontiguousarray(np.concatenate(
        [blocks(a["L1_xattn_Wq"].T), blocks(a["L1_xattn_Wout"].T), kv], axis=1))
    names = (("Wup", "Wsu"), ("Wgate", "Wsg"), ("Wdown", "Wsd"))
    arrays["w_exp"] = np.ascontiguousarray(np.stack(
        [[blocks(w) for w in (a["L1_ffn_" + n][e] if e < E else a["L1_ffn_" + m] for n, m in names)]
         for e in range(EA)], 0))
    bias = np.stack([np.concatenate([a["L1_ffn_" + n], a["L1_ffn_" + m][None]], 0)
                     for n, m in (("bup", "bsu"), ("bgate", "bsg"))], 1)
    arrays["b_exp"] = np.ascontiguousarray(bias.reshape(EA, 2, KC, 128).transpose(3, 0, 1, 2))
    arrays["b_down"] = np.ascontiguousarray(np.concatenate([a["L1_ffn_bdown"], a["L1_ffn_bsd"][None]], 0))
    wr = np.zeros((D, EA), np.float32)
    wr[:, :E] = a["L1_ffn_Wr"]
    arrays["w_router"] = np.ascontiguousarray(wr.reshape(KC, 128, EA).transpose(1, 0, 2))
    arrays["b_router"] = np.ascontiguousarray(np.stack([a["L1_ffn_br"], a["L1_ffn_gate_bias"]], 0))
    arrays["order"] = np.arange(E, 0, -1).astype(np.float32)
    return arrays


def kernel(**inputs):
    import numpy as np
    import concourse.bacc as bacc
    from concourse.bass_utils import run_bass_kernel_spmd

    nc = bacc.Bacc("TRN2", target_bir_lowering=False, num_devices=1)
    arrays = layouts(np, inputs)
    aps = {name: nc.dram_tensor(name, a.shape, mybir.dt.from_np(a.dtype), kind="ExternalInput").ap()
           for name, a in arrays.items()}
    out = nc.dram_tensor("out", (B, S, D), F32, kind="ExternalOutput").ap()
    build(nc, out=out, **aps)
    return run_bass_kernel_spmd(nc, [arrays], core_ids=[0]).results[0]["out"]
```
